# Optimizing a Trainium2 kernel written in Bass

```python
import numpy as np
import jax
import jax.numpy as jnp

def _softmax(x, axis=-1):
    return jax.nn.softmax(x, axis=axis)

def _gelu(x):
    return jax.nn.gelu(x, approximate=True)

def _silu(x):
    return jax.nn.silu(x)

def _sigmoid(x):
    return jax.nn.sigmoid(x)

def _layernorm(x, axis=-1, eps=1e-05):
    m = jnp.mean(x, axis=axis, keepdims=True)
    v = jnp.var(x, axis=axis, keepdims=True)
    return (x - m) / jnp.sqrt(v + eps)

def _scatter_add(tgt, idx, src, axis=0):
    return tgt.at[idx].add(src)

def _segment_sum(src, seg, n):
    return jax.ops.segment_sum(src, seg, n)
kernel_name = 'mk_adaln_d1_jaxref_r8_f7d8bc'

def setup_inputs(seed: int=0):
    np.random.seed(seed)
    _w = jnp.asarray

    def _L0_attn_setup():
        import jax, jax.numpy as jnp
        import numpy as np
        DECAY = 0.9
        key = jax.random.key(seed)
        ks = jax.random.split(key, 8)
        B, L, d_model = (4, 256, 128)
        d_state = 16
        d_inner = 2 * d_model
        x = jax.random.normal(ks[0], (B, L, d_model), dtype=jnp.float32)
        Win = jax.random.normal(ks[1], (d_model, d_inner), dtype=jnp.float32) / np.sqrt(d_model)
        bin_ = jnp.zeros((d_inner,), dtype=jnp.float32)
        Bp = jax.random.normal(ks[2], (d_inner, d_state), dtype=jnp.float32) * 0.01
        Cp = jax.random.normal(ks[3], (d_state, d_inner), dtype=jnp.float32) * 0.01
        Dp = jnp.ones((d_inner,), dtype=jnp.float32)
        Wout = jax.random.normal(ks[4], (d_inner, d_model), dtype=jnp.float32) / np.sqrt(d_inner)
        bout = jnp.zeros((d_model,), dtype=jnp.float32)
        return {'x': x, 'Win': Win, 'bin_': bin_, 'Bp': Bp, 'Cp': Cp, 'Dp': Dp, 'Wout': Wout, 'bout': bout}
    _L0_attn_in = _L0_attn_setup()

    def _L0_ffn_setup():
        import jax, jax.numpy as jnp
        import numpy as np
        E = 8
        K = 2
        D = 128
        F = 512
        EPS = 1e-05

        def _layernorm(h, g, b):
            mu = h.mean(axis=-1, keepdims=True)
            var = ((h - mu) ** 2).mean(axis=-1, keepdims=True)
            return (h - mu) * jax.lax.rsqrt(var + EPS) * g[:, None, :] + b[:, None, :]
        key = jax.random.key(seed)
        ks = jax.random.split(key, 8)
        B, S = (2, 256)
        x = jax.random.normal(ks[0], (B, S, D), dtype=jnp.float32)
        Wr = jax.random.normal(ks[1], (D, E), dtype=jnp.float32) / np.sqrt(D)
        br = jnp.zeros((E,), dtype=jnp.float32)
        W1 = jax.random.normal(ks[2], (E, D, F), dtype=jnp.float32) / np.sqrt(D)
        b1 = jnp.zeros((E, F), dtype=jnp.float32)
        g1 = jnp.ones((E, F), dtype=jnp.float32)
        be1 = jnp.zeros((E, F), dtype=jnp.float32)
        W2 = jax.random.normal(ks[3], (E, F, D), dtype=jnp.float32) / np.sqrt(F)
        b2 = jnp.zeros((E, D), dtype=jnp.float32)
        g2 = jnp.ones((E, D), dtype=jnp.float32)
        be2 = jnp.zeros((E, D), dtype=jnp.float32)
        return {'x': x, 'Wr': Wr, 'br': br, 'W1': W1, 'b1': b1, 'g1': g1, 'be1': be1, 'W2': W2, 'b2': b2, 'g2': g2, 'be2': be2}
    _L0_ffn_in = _L0_ffn_setup()
    _L0_c = _w((lambda *s: np.random.randn(*s).astype(np.float32) * 0.05)(16, 128))
    _L0_wmod = _w((lambda *s: np.random.randn(*s).astype(np.float32) * 0.05)(128, 6 * 128) * 128 ** (-0.5))
    _d = {'L0_attn_x': _L0_attn_in['x'], 'L0_attn_Win': _L0_attn_in['Win'], 'L0_attn_bin_': _L0_attn_in['bin_'], 'L0_attn_Bp': _L0_attn_in['Bp'], 'L0_attn_Cp': _L0_attn_in['Cp'], 'L0_attn_Dp': _L0_attn_in['Dp'], 'L0_attn_Wout': _L0_attn_in['Wout'], 'L0_attn_bout': _L0_attn_in['bout'], 'L0_ffn_Wr': _L0_ffn_in['Wr'], 'L0_ffn_br': _L0_ffn_in['br'], 'L0_ffn_W1': _L0_ffn_in['W1'], 'L0_ffn_b1': _L0_ffn_in['b1'], 'L0_ffn_g1': _L0_ffn_in['g1'], 'L0_ffn_be1': _L0_ffn_in['be1'], 'L0_ffn_W2': _L0_ffn_in['W2'], 'L0_ffn_b2': _L0_ffn_in['b2'], 'L0_ffn_g2': _L0_ffn_in['g2'], 'L0_ffn_be2': _L0_ffn_in['be2'], 'L0_c': _L0_c, 'L0_wmod': _L0_wmod}
    _x0 = _d['L0_attn_x']
    _d['L0_attn_x'] = jax.random.normal(jax.random.fold_in(jax.random.key(seed), 1), (16, 512, 128), dtype=_x0.dtype)
    del _x0
    return _d

def reference(L0_attn_x, L0_attn_Win, L0_attn_bin_, L0_attn_Bp, L0_attn_Cp, L0_attn_Dp, L0_attn_Wout, L0_attn_bout, L0_ffn_Wr, L0_ffn_br, L0_ffn_W1, L0_ffn_b1, L0_ffn_g1, L0_ffn_be1, L0_ffn_W2, L0_ffn_b2, L0_ffn_g2, L0_ffn_be2, L0_c, L0_wmod):

    def _L0_attn_ref(x, Win, bin_, Bp, Cp, Dp, Wout, bout):
        import jax, jax.numpy as jnp
        import numpy as np
        DECAY = 0.9
        B, L, _ = x.shape
        d_inner, d_state = Bp.shape
        xi = jax.nn.silu(x @ Win + bin_)
        xt_seq = jnp.swapaxes(xi, 0, 1)

        def step(h, xt):
            h = h * DECAY + xt[:, :, None] * Bp[None, :, :]
            y = jnp.einsum('bij,ji->bi', h, Cp) + Dp * xt
            return (h, y)
        h0 = jnp.zeros((B, d_inner, d_state), dtype=x.dtype)
        _, ys = jax.lax.scan(step, h0, xt_seq)
        y = jnp.swapaxes(ys, 0, 1)
        return y @ Wout + bout

    def _L0_ffn_ref(x, Wr, br, W1, b1, g1, be1, W2, b2, g2, be2):
        import jax, jax.numpy as jnp
        import numpy as np
        E = 8
        K = 2
        D = 128
        F = 512
        EPS = 1e-05

        def _layernorm(h, g, b):
            mu = h.mean(axis=-1, keepdims=True)
            var = ((h - mu) ** 2).mean(axis=-1, keepdims=True)
            return (h - mu) * jax.lax.rsqrt(var + EPS) * g[:, None, :] + b[:, None, :]
        B, S, _ = x.shape
        xt = x.reshape(-1, D)
        logits = xt @ Wr + br
        p = jax.nn.softmax(logits, axis=-1)
        probs, idx = jax.lax.top_k(p, K)
        probs = probs / probs.sum(axis=-1, keepdims=True)
        h = jnp.einsum('td,edf->etf', xt, W1) + b1[:, None, :]
        h = _layernorm(jax.nn.relu(h), g1, be1)
        y = jnp.einsum('etf,efd->etd', h, W2) + b2[:, None, :]
        y = _layernorm(jax.nn.relu(y), g2, be2)
        gate = (jax.nn.one_hot(idx, E, dtype=x.dtype) * probs[..., None]).sum(axis=1)
        out = jnp.einsum('te,etd->td', gate, y)
        return out.reshape(B, S, D)
    x = L0_attn_x
    mod = (_silu(L0_c) @ L0_wmod).reshape(L0_c.shape[0], 6, 1, -1)
    sa, ca, ga, sb, cb, gb = (mod[:, 0], mod[:, 1], mod[:, 2], mod[:, 3], mod[:, 4], mod[:, 5])
    ga = (2 * (ga >= 0) - 1) * jnp.maximum(jnp.abs(ga), 0.25)
    gb = (2 * (gb >= 0) - 1) * jnp.maximum(jnp.abs(gb), 0.25)
    h = _layernorm(x, axis=-1) * (1 + ca) + sa
    x = x + ga * _L0_attn_ref(h, L0_attn_Win, L0_attn_bin_, L0_attn_Bp, L0_attn_Cp, L0_attn_Dp, L0_attn_Wout, L0_attn_bout)
    h = _layernorm(x, axis=-1) * (1 + cb) + sb
    x = x + gb * _L0_ffn_ref(h, L0_ffn_Wr, L0_ffn_br, L0_ffn_W1, L0_ffn_b1, L0_ffn_g1, L0_ffn_be1, L0_ffn_W2, L0_ffn_b2, L0_ffn_g2, L0_ffn_be2)
    return x

_drawn_inputs = setup_inputs


def setup_inputs(seed=0):
    import zlib

    import numpy as np

    out = dict(_drawn_inputs(seed))
    spreads = {'L0_attn_bin_': (0.0, 0.301),
     'L0_attn_Dp': (1.0, 0.2),
     'L0_attn_bout': (0.0, 0.1),
     'L0_ffn_br': (0.0, 0.1),
     'L0_ffn_b1': (0.0, 0.3),
     'L0_ffn_g1': (1.0, 0.2),
     'L0_ffn_be1': (0.0, 0.363),
     'L0_ffn_b2': (0.0, 0.376),
     'L0_ffn_g2': (1.0, 0.2),
     'L0_ffn_be2': (0.0, 0.451)}
    factors = {'L0_attn_Bp': 8.0, 'L0_attn_Cp': 8.0}
    for name, (base, spread) in spreads.items():
        noise = np.random.default_rng([zlib.crc32(name.encode()), seed]).standard_normal(out[name].shape)
        drawn = base * np.exp(spread * noise) if base else spread * noise
        out[name] = jnp.asarray(drawn.astype(out[name].dtype))
    for name, factor in factors.items():
        out[name] = (out[name] * factor).astype(out[name].dtype)
    return out
```

```python
from contextlib import ExitStack

import concourse.bass as bass
from concourse import mybir


def adaln_ssm_moe_kernel(nc, x_in, win_in, bin_in, bp_in, cp_in, dp_in, wout_in, bout_in, wr_in, br_in,
                         w1_in, b1_in, g1_in, be1_in, w2_in, b2_in, g2_in, be2_in, c_in, wmod_in, out):
    F32, F32R, BF16 = mybir.dt.float32, mybir.dt.float32r, mybir.dt.bfloat16
    I32, U32 = mybir.dt.int32, mybir.dt.uint32
    ALU = mybir.AluOpType
    ACT = mybir.ActivationFunctionType
    AX = mybir.AxisListType.X

    B, L, D = x_in.shape
    P = 128
    J = L // P
    T = B * L
    NT = T // P
    DI, NS = bp_in.shape
    CI = DI // P
    E, _, F = w1_in.shape
    CF = F // P
    TOPK = 2
    EPS = 1e-5
    DECAY = 0.9
    REGION = T + P
    EXPERT_TILES = TOPK * NT + E
    SPARE = E * REGION
    NSPARE = EXPERT_TILES - TOPK * NT
    ROW = D + 2
    NOWHERE = 65536.0
    assert D == P and EXPERT_TILES % 2 == 0 and B % 2 == 0

    x_v = x_in.rearrange("b l d -> (b l) d").rearrange("(n p) d -> p n d", p=P)
    out_v = out.rearrange("b l d -> (b l) d").rearrange("(n p) d -> p n d", p=P)
    rows_d = nc.dram_tensor("expert_rows", (SPARE + NSPARE * P, ROW), F32, kind="Internal").ap()
    results_d = nc.dram_tensor("expert_results", (TOPK * T, D), F32, kind="Internal").ap()
    results_v = results_d.rearrange("(n p k) d -> p n (k d)", p=P, k=TOPK)
    gates_d = nc.dram_tensor("gate_b_rows", (1, B * D), F32, kind="Internal").ap()

    with ExitStack() as ctx:
        def sb(name, shape, dt=F32):
            return ctx.enter_context(nc.sbuf_tensor(name, shape, dt))

        def sem(name):
            return ctx.enter_context(nc.semaphore(name))

        bank = [ctx.enter_context(nc.psum_tensor(f"bank{n}", [P, 512], F32)) for n in range(8)]

        X = sb("X", [P, NT, D])
        W1 = sb("W1", [P, E, F])
        W2 = sb("W2", [P, E * CF, D])
        c2 = sb("c2", [P, E, D])
        g2 = sb("g2", [P, E, D])
        be2 = sb("be2", [P, E, D])
        gb_rows = sb("gb_rows", [P, B, D])
        win = sb("win", [P, DI])
        wout = sb("wout", [P, CI, D])
        wz = sb("wz", [P, CI, D])
        wu = sb("wu", [P, CI, D])
        wr = sb("wr", [P, E])
        br = sb("br", [P, E])
        wmod = sb("wmod", [P, 6 * D])
        bcol = sb("bcol", [P, CI])
        dcol = sb("dcol", [P, CI])
        boutc = sb("boutc", [P, 1])
        bp = sb("bp", [P, CI, NS])
        cp = sb("cp", [NS, DI])
        cpT = sb("cpT", [P, CI, NS])
        ccol = sb("ccol", [P, CI])
        c_sb = sb("c_sb", [B, D])
        c_act = sb("c_act", [B, D])
        cT = sb("cT", [P, B])
        mod = sb("mod", [P, 5, B])
        mod_sign = sb("mod_sign", [P, B])
        mod_abs = sb("mod_abs", [P, B])
        ga_bout = sb("ga_bout", [P, B])
        gb_raw = sb("gb_raw", [B, D])
        gb_sign = sb("gb_sign", [B, D])
        gb_abs = sb("gb_abs", [B, D])
        g1r = sb("g1r", [E * CF, P])
        be1r = sb("be1r", [E * CF, P])
        g1T = sb("g1T", [P, E * CF])
        be1T = sb("be1T", [P, E * CF])
        b1f = sb("b1f", [E, F])
        b1hi = sb("b1hi", [E, F], F32R)
        b1lo = sb("b1lo", [E, F], F32R)
        b1_parts = sb("b1_parts", [2, E, F], F32R)
        onesr = sb("onesr", [2, P], F32R)
        onesf = sb("onesf", [2, P])
        offs = sb("offs", [P, P], I32)
        ident = sb("ident", [P, P])
        before = sb("before", [P, P], BF16)
        ones = sb("ones", [P, P], BF16)
        mean_w = sb("mean_w", [P, P])
        decay = sb("decay", [P, L])
        eps = sb("eps", [P, 1])
        minus_half = sb("minus_half", [P, J])
        iota_e = sb("iota_e", [P, E])
        iota_ei = sb("iota_ei", [P, E], I32)
        base_e = sb("base_e", [P, E])
        token_i = sb("token_i", [P, NT], I32)
        token = sb("token", [P, NT])
        padding = sb("padding", [P, ROW])
        st1 = sb("st1", [P, NT, 6])
        mv1 = sb("mv1", [P, NT, 2])
        sd1 = sb("sd1", [P, NT])
        rs1 = sb("rs1", [P, NT])
        nm1 = sb("nm1", [P, NT])
        lead = sb("lead", [P, NT])
        n1 = [sb(f"n1_{q}", [P, J, D]) for q in range(2)]
        h1T = [sb(f"h1T_{q}", [P, L]) for q in range(2)]
        xi = [sb(f"xi_{q}", [P, CI, L]) for q in range(2)]
        scan = [sb(f"scan_{q}", [P, L]) for q in range(2)]
        skip = [sb(f"skip_{q}", [P, L]) for q in range(2)]
        mixT = [sb(f"mixT_{q}", [P, L]) for q in range(2)]
        st2 = [sb(f"st2_{q}", [P, J, 6]) for q in range(2)]
        mv2 = [sb(f"mv2_{q}", [P, J, 2]) for q in range(2)]
        ve2 = [sb(f"ve2_{q}", [P, J]) for q in range(2)]
        rs2 = [sb(f"rs2_{q}", [P, J]) for q in range(2)]
        n2 = [sb(f"n2_{q}", [P, J, D]) for q in range(2)]
        h2T = [sb(f"h2T_{q}", [P, L]) for q in range(2)]
        rows = [sb(f"rows_{q}", [P, J, ROW]) for q in range(2)]
        logit = [sb(f"logit_{q}", [P, J, E]) for q in range(2)]
        best = [sb(f"best_{q}", [P, J, 8]) for q in range(2)]
        besti = [sb(f"besti_{q}", [P, J, 8], U32) for q in range(2)]
        hot = [sb(f"hot_{q}", [P, J, TOPK, E]) for q in range(2)]
        hots = [sb(f"hots_{q}", [P, J, E], BF16) for q in range(2)]
        hotsum = [sb(f"hotsum_{q}", [P, E]) for q in range(2)]
        carry = sb("carry", [P, E], BF16)
        place = [sb(f"place_{q}", [P, J, E]) for q in range(2)]
        placed = [sb(f"placed_{q}", [P, J, TOPK, E]) for q in range(2)]
        slot = [sb(f"slot_{q}", [P, J, TOPK], I32) for q in range(2)]
        cnt = sb("cnt", [P, E])
        cnt_i = sb("cnt_i", [P, E], I32)
        nt_i = sb("nt_i", [P, E], I32)
        nt_f = sb("nt_f", [P, E])
        ends = sb("ends", [P, E])
        ones_e = sb("ones_e", [P, E])
        jump = sb("jump", [P, E])
        it_i = sb("it_i", [P, EXPERT_TILES], I32)
        it_f = sb("it_f", [P, EXPERT_TILES])
        past = sb("past", [P, E, EXPERT_TILES])
        hop = sb("hop", [P, E, EXPERT_TILES])
        tile_e = sb("tile_e", [P, EXPERT_TILES])
        tile_hop = sb("tile_hop", [P, EXPERT_TILES])
        tile_ei = sb("tile_ei", [P, EXPERT_TILES], I32)
        tile_row = sb("tile_row", [P, EXPERT_TILES], I32)
        hrow = [sb(f"hrow_{q}", [P, ROW]) for q in range(2)]
        h3T = [sb(f"h3T_{q}", [P, P]) for q in range(2)]
        r = h1T
        rT = h2T
        stf = [sb(f"stf_{q}", [P, 6]) for q in range(2)]
        mvf = [sb(f"mvf_{q}", [P, 2]) for q in range(2)]
        sdf = [sb(f"sdf_{q}", [P, 1]) for q in range(2)]
        rsf = [sb(f"rsf_{q}", [P, 1]) for q in range(2)]
        v0 = [sb(f"v0_{q}", [P, D]) for q in range(2)]
        v = [sb(f"v_{q}", [P, D]) for q in range(2)]
        sty = [sb(f"sty_{q}", [P, 6]) for q in range(2)]
        mvy = [sb(f"mvy_{q}", [P, 2]) for q in range(2)]
        sdy = [sb(f"sdy_{q}", [P, 1]) for q in range(2)]
        rsy = [sb(f"rsy_{q}", [P, 1]) for q in range(2)]
        vg = [sb(f"vg_{q}", [P, D]) for q in range(2)]
        y = [sb(f"y_{q}", [P, D]) for q in range(2)]
        targets = sb("targets", [P, EXPERT_TILES], I32)
        target = [sb(f"target_{q}", [P, 1], I32) for q in range(2)]
        gate = sb("gate", [P, TOPK, NT])
        y01 = [t[:, :, :].rearrange("p c (j k) -> p (c j) k", k=TOPK * D) for t in xi]
        y0g = n1
        ysum = n2
        ygb = [t[:, :].rearrange("p (j d) -> p j d", j=J) for t in scan]
        o = [t[:, :].rearrange("p (j d) -> p j d", j=J) for t in skip]

        XL = 4
        x_loaded = [sem(f"x_loaded{n}") for n in range(XL)]
        small_loaded = sem("small_loaded")
        mod_loaded = sem("mod_loaded")
        w1_loaded, w2_loaded, rows_loaded = sem("w1_loaded"), sem("w2_loaded"), sem("rows_loaded")
        spare_stored = sem("spare_stored")
        pool_consts = sem("pool_consts")
        dve_setup, act_setup, pe_setup = sem("dve_setup"), sem("act_setup"), sem("pe_setup")
        gb_stored, gb_loaded, b1_stored = sem("gb_stored"), sem("gb_loaded"), sem("b1_stored")
        (n1_ready, t1_done, h1T_ready, xi0_done, xi1_done, xi0_ready, xi1_ready, z_done, u_done, skip_ready,
         scan_ready, mix_ready, mix_done) = [sem(n) for n in (
             "n1_ready", "t1_done", "h1T_ready", "xi0_done", "xi1_done", "xi0_ready", "xi1_ready", "z_done",
             "u_done", "skip_ready", "scan_ready", "mix_ready", "mix_done")]
        (x1_ready, st2_ready, mv2_ready, ve2_ready, rs2_ready, n2_ready, t2_done, h2T_ready, back_done,
         logit_done, rows_ready, logit_ready, best_ready, besti_ready, hot_ready, hots_ready, carry_ready,
         rank_done, place_ready, placed_ready, slot_ready, hotsum_ready) = [sem(n) for n in (
             "x1_ready", "st2_ready", "mv2_ready", "ve2_ready", "rs2_ready", "n2_ready", "t2_done", "h2T_ready",
             "back_done", "logit_done", "rows_ready", "logit_ready", "best_ready", "besti_ready", "hot_ready",
             "hots_ready", "carry_ready", "rank_done", "place_ready", "placed_ready", "slot_ready",
             "hotsum_ready")]
        rows_stored = [sem(f"rows_stored{q}") for q in range(2)]
        count_done, table_step, table_ready, padding_stored = (
            sem("count_done"), sem("table_step"), sem("table_ready"), sem("padding_stored"))
        hrow_loaded = [sem(f"hrow_loaded{q}") for q in range(2)]
        (t3_done, h3T_ready, h_done, r_ready, tr_done, rT_ready, y_done, stf_ready, mvf_ready, sdf_ready,
         rsf_ready, v0_ready, v_ready, sty_ready, mvy_ready, sdy_ready, rsy_ready, vg_ready, y_ready,
         targets_ready, target_ready) = [sem(n) for n in (
             "t3_done", "h3T_ready", "h_done", "r_ready", "tr_done", "rT_ready", "y_done", "stf_ready",
             "mvf_ready", "sdf_ready", "rsf_ready", "v0_ready", "v_ready", "sty_ready", "mvy_ready", "sdy_ready",
             "rsy_ready", "vg_ready", "y_ready", "targets_ready", "target_ready")]
        results_stored = [sem(f"results_stored{q}") for q in range(2)]
        gate_ready = sem("gate_ready")
        y01_loaded = [sem(f"y01_loaded{q}") for q in range(2)]
        y0g_ready, ysum_ready, ygb_ready, o_ready = (
            sem("y0g_ready"), sem("ysum_ready"), sem("ygb_ready"), sem("o_ready"))
        out_stored = [sem(f"out_stored{q}") for q in range(2)]

        block = ctx.enter_context(nc.Block())

        HALF = EXPERT_TILES // 2

        def tiles(b):
            return bass.ds(b * J, J)

        @block.sync
        def _(sp):
            sp.dma_start(c_sb[:], c_in).then_inc(mod_loaded, 16)
            sp.dma_start(wmod[:], wmod_in).then_inc(mod_loaded, 16)
            NX = NT // XL
            sp.dma_start(X[:, 0:NX, :], x_v[:, 0:NX, :]).then_inc(x_loaded[0], 16)
            sp.dma_start(win[:], win_in).then_inc(small_loaded, 16)
            sp.dma_start(wout[:], wout_in.rearrange("(c p) d -> p c d", p=P)).then_inc(small_loaded, 16)
            sp.dma_start(bp[:], bp_in.rearrange("(c p) s -> p c s", p=P)).then_inc(small_loaded, 16)
            sp.dma_start(cp[:], cp_in).then_inc(small_loaded, 16)
            sp.dma_start(bcol[:], bin_in.rearrange("(c p) -> p c", p=P), allow_slow_non_contiguous=True).then_inc(small_loaded, 16)
            sp.dma_start(dcol[:], dp_in.rearrange("(c p) -> p c", p=P), allow_slow_non_contiguous=True).then_inc(small_loaded, 16)
            sp.dma_start(boutc[:], bout_in.rearrange("(p o) -> p o", o=1), allow_slow_non_contiguous=True).then_inc(small_loaded, 16)
            sp.dma_start(wr[:], wr_in).then_inc(small_loaded, 16)
            sp.dma_start(br[:], br_in.rearrange("(o e) -> o e", o=1).broadcast_to([P, E])).then_inc(small_loaded, 16)
            for n in range(1, XL):
                sp.dma_start(X[:, n * NX:(n + 1) * NX, :], x_v[:, n * NX:(n + 1) * NX, :]).then_inc(x_loaded[n], 16)
            sp.dma_start(W2[:], w2_in.rearrange("e (c p) d -> p (e c) d", p=P)).then_inc(w2_loaded, 16)
            sp.dma_start(g1r[:], g1_in.rearrange("e (c p) -> (e c) p", p=P)).then_inc(w2_loaded, 16)
            sp.dma_start(be1r[:], be1_in.rearrange("e (c p) -> (e c) p", p=P)).then_inc(w2_loaded, 16)
            sp.dma_start(b1f[:], b1_in).then_inc(w2_loaded, 16)
            for dst, src in ((c2, b2_in), (g2, g2_in), (be2, be2_in)):
                sp.dma_start(dst[:], src.rearrange("(o e) d -> o e d", o=1).broadcast_to([P, E, D])).then_inc(rows_loaded, 16)
            sp.dma_start(W1[:], w1_in.rearrange("e p f -> p e f")).then_inc(w1_loaded, 16)
            sp.wait_ge(dve_setup, SETUP_GB)
            sp.dma_start(gates_d.rearrange("o (b d) -> (o b) d", b=B), gb_raw[:]).then_inc(gb_stored, 16)
            sp.wait_ge(gb_stored, 16)
            sp.dma_start(gb_rows[:], gates_d.rearrange("o (b d) -> o b d", b=B).broadcast_to([P, B, D])).then_inc(gb_loaded, 16)
            sp.wait_ge(dve_setup, SETUP_B1LO)
            sp.wait_ge(act_setup, 3)
            sp.dma_start(b1_parts[0:1, :, :].bitcast(F32), b1hi[:].bitcast(F32)).then_inc(b1_stored, 16)
            sp.dma_start(b1_parts[1:2, :, :].bitcast(F32), b1lo[:].bitcast(F32)).then_inc(b1_stored, 16)
            sp.wait_ge(dve_setup, SETUP_PADDING)
            for n in range(NSPARE):
                sp.dma_start(rows_d[SPARE + n * P:SPARE + (n + 1) * P, :], padding[:]).then_inc(spare_stored, 16)
            sp.wait_ge(table_ready, 1)
            for e in range(E):
                n = sp.value_load(cnt_i[0:1, e:e + 1], min_val=0, max_val=T)
                sp.dma_start(rows_d[bass.ds(n + e * REGION, P), :], padding[:]).then_inc(padding_stored, 16)
            sp.wait_ge(spare_stored, 16 * NSPARE)
            sp.wait_ge(padding_stored, 16 * E)
            for q in range(2):
                sp.wait_ge(rows_stored[q], 16 * J * TOPK * (B // 2))

            def load_rows(i, q, first):
                start = sp.value_load(tile_row[0:1, bass.ds(i, 1)], min_val=0, max_val=SPARE + (NSPARE - 1) * P)
                if not first:
                    sp.wait_ge(t3_done, i - 1)
                    sp.wait_ge(targets_ready, i - 1)
                sp.dma_start(hrow[q][:], rows_d[bass.ds(start, P), :]).then_inc(hrow_loaded[q], 16)

            for q in range(2):
                load_rows(q, q, True)
            with sp.Fori(2, EXPERT_TILES - 1, 2) as i:
                for q in range(2):
                    load_rows(i + q, q, False)
            for q in range(2):
                sp.wait_ge(results_stored[q], 16 * HALF)

            def load_results(b, q):
                sp.dma_start(y01[q], results_v[:, tiles(b), :]).then_inc(y01_loaded[q], 16)

            def store_out(b, q):
                sp.wait_ge(o_ready, b + 1)
                sp.dma_start(out_v[:, tiles(b), :], o[q][:]).then_inc(out_stored[q], 16)

            for q in range(2):
                load_results(q, q)
            with sp.Fori(2, B - 1, 2) as b:
                for q in range(2):
                    store_out(b + q - 2, q)
                    load_results(b + q, q)
            for q in range(2):
                store_out(B - 2 + q, q)
            for q in range(2):
                sp.wait_ge(out_stored[q], 16 * (B // 2))

        @block.gpsimd
        def _(pool):
            nc.gpsimd.iota(offs[:], pattern=[[1, P]], base=0, channel_multiplier=-1).then_inc(pool_consts, 1)
            nc.gpsimd.iota(iota_ei[:], pattern=[[1, E]], base=0, channel_multiplier=0).then_inc(pool_consts, 1)
            nc.gpsimd.iota(token_i[:], pattern=[[TOPK * P, NT]], base=0, channel_multiplier=TOPK).then_inc(pool_consts, 1)
            nc.gpsimd.iota(it_i[:], pattern=[[1, EXPERT_TILES]], base=0, channel_multiplier=0).then_inc(pool_consts, 1)
            nc.gpsimd.memset(decay[:], DECAY).then_inc(pool_consts, 1)
            nc.gpsimd.memset(minus_half[:], -0.5).then_inc(pool_consts, 1)
            nc.gpsimd.memset(mean_w[:], 1.0 / F).then_inc(pool_consts, 1)
            nc.gpsimd.memset(ones[:], 1.0).then_inc(pool_consts, 1)
            pool.wait_ge(pool_consts, 8)

            def inverse_deviation(b, q):
                pool.wait_ge(ve2_ready, b + 1)
                nc.gpsimd.tensor_tensor(rs2[q][:], ve2[q][:], minus_half[:], ALU.pow).then_inc(rs2_ready, 1)

            def store_rows(b, q):
                pool.wait_ge(rows_ready, b + 1)
                pool.wait_ge(slot_ready, b + 1)
                pool.nop(nofuse=True)
                for j in range(J):
                    for k in range(TOPK):
                        nc.gpsimd.indirect_dma_start(
                            out=rows_d, out_offset=bass.IndirectOffsetOnAxis(ap=slot[q][:, j, k:k + 1], axis=0),
                            in_=rows[q][:, j, :], in_offset=None).then_inc(rows_stored[q], 16)

            inverse_deviation(0, 0)
            with pool.Fori(1, B - 2, 2) as b:
                inverse_deviation(b, 1)
                store_rows(b - 1, 0)
                inverse_deviation(b + 1, 0)
                store_rows(b, 1)
            inverse_deviation(B - 1, 1)
            store_rows(B - 2, 0)
            store_rows(B - 1, 1)

            def store_results(i, q, first):
                pool.wait_ge(targets_ready, i + 1)
                if not first:
                    pool.wait_ge(results_stored[q], (i - q) * 8)
                nc.gpsimd.tensor_copy(target[q][:], targets[:, bass.ds(i, 1)]).then_inc(target_ready, 1)
                pool.wait_ge(target_ready, i + 1)
                pool.wait_ge(y_ready, i + 1)
                pool.nop(nofuse=True)
                nc.gpsimd.indirect_dma_start(
                    out=results_d, out_offset=bass.IndirectOffsetOnAxis(ap=target[q][:], axis=0),
                    in_=y[q][:], in_offset=None, bounds_check=TOPK * T - 1, oob_is_err=False,
                ).then_inc(results_stored[q], 16)

            for q in range(2):
                store_results(q, q, True)
            with pool.Fori(2, EXPERT_TILES - 1, 2) as i:
                for q in range(2):
                    store_results(i + q, q, False)

        @block.scalar
        def _(act):
            act.wait_ge(mod_loaded, 32)
            nc.scalar.activation(c_act[:], c_sb[:], ACT.Silu).then_inc(act_setup, 1)
            act.wait_ge(dve_setup, SETUP_MV1)
            nc.scalar.activation(sd1[:], mv1[:, :, 1], ACT.Sqrt, bias=eps[:]).then_inc(act_setup, 1)
            act.wait_ge(w2_loaded, 64)
            nc.scalar.activation(b1hi[:], b1f[:], ACT.Copy).then_inc(act_setup, 1)
            nc.scalar.activation(onesr[:], onesf[:], ACT.Copy).then_inc(act_setup, 1)
            act.wait_ge(dve_setup, SETUP_END)

            def normalise1(b, q):
                for j in range(J):
                    ins = nc.scalar.activation(n1[q][:, j:j + 1, :], X[:, bass.ds(b * J + j, 1), :], ACT.Identity,
                                               bias=nm1[:, bass.ds(b * J + j, 1)], scale=rs1[:, bass.ds(b * J + j, 1)])
                ins.then_inc(n1_ready, 1)

            def mixer(b, q):
                act.wait_ge(t1_done, b + 1)
                nc.scalar.activation(h1T[q][:], bank[0][:], ACT.Identity, bias=mod[:, 0, bass.ds(b, 1)],
                                     scale=mod[:, 1, bass.ds(b, 1)]).then_inc(h1T_ready, 1)
                act.wait_ge(xi0_done, b + 1)
                nc.scalar.activation(xi[q][:, 0, :], bank[1][:], ACT.Silu, bias=bcol[:, 0:1]).then_inc(xi0_ready, 1)
                act.wait_ge(xi1_done, b + 1)
                nc.scalar.activation(xi[q][:, 1, :], bank[2][:], ACT.Silu, bias=bcol[:, 1:2]).then_inc(xi1_ready, 1)

            def modulate2(b, q):
                act.wait_ge(t2_done, b + 1)
                nc.scalar.activation(h2T[q][:], bank[6][:], ACT.Identity, bias=mod[:, 3, bass.ds(b, 1)],
                                     scale=mod[:, 4, bass.ds(b, 1)]).then_inc(h2T_ready, 1)

            def skip_path(b, q):
                act.wait_ge(u_done, b + 1)
                nc.scalar.activation(skip[q][:], bank[4][:], ACT.Identity, bias=ga_bout[:, bass.ds(b, 1)],
                                     scale=mod[:, 2, bass.ds(b, 1)]).then_inc(skip_ready, 1)

            def keep_rows(b, q, stored):
                act.wait_ge(back_done, b + 1)
                if stored is not None:
                    act.wait_ge(rows_stored[q], stored)
                nc.scalar.activation(rows[q][:, :, 0:D], bank[6][:].rearrange("p (j d) -> p j d", j=J),
                                     ACT.Copy).then_inc(rows_ready, 1)

            def step(b, q, stored, last=False):
                mixer(b, q)
                modulate2(b - 1, 1 - q)
                skip_path(b, q)
                keep_rows(b - 1, 1 - q, stored)
                if not last:
                    normalise1(b + 1, 1 - q)

            per = 16 * J * TOPK
            normalise1(0, 0)
            mixer(0, 0)
            skip_path(0, 0)
            normalise1(1, 1)
            step(1, 1, None)
            step(2, 0, None)
            with act.Fori(3, B - 2, 2) as b:
                step(b, 1, (b - 1) * (per // 2))
                step(b + 1, 0, (b - 1) * (per // 2))
            step(B - 1, 1, (B - 2) // 2 * per, last=True)
            modulate2(B - 1, 1)
            keep_rows(B - 1, 1, (B - 2) // 2 * per)

            def rows_T(i, q):
                act.wait_ge(t3_done, i + 1)
                nc.scalar.activation(h3T[q][:], bank[0][:, 0:P], ACT.Copy).then_inc(h3T_ready, 1)

            def hidden_T(i, q):
                act.wait_ge(tr_done, i + 1)
                nc.scalar.activation(rT[q][:], bank[3][:], ACT.Copy).then_inc(rT_ready, 1)

            def deviation_h(i, q):
                act.wait_ge(mvf_ready, i + 1)
                nc.scalar.activation(sdf[q][:], mvf[q][:, 1:2], ACT.Sqrt, bias=eps[:]).then_inc(sdf_ready, 1)

            def deviation_y(i, q):
                act.wait_ge(mvy_ready, i + 1)
                nc.scalar.activation(sdy[q][:], mvy[q][:, 1:2], ACT.Sqrt, bias=eps[:]).then_inc(sdy_ready, 1)

            def hidden(i, q):
                act.wait_ge(h_done, i + 1)
                nc.scalar.activation(r[q][:], bank[1 + q][:], ACT.Relu).then_inc(r_ready, 1)

            def relu_y(i, q):
                act.wait_ge(v0_ready, i + 1)
                nc.scalar.activation(v[q][:], v0[q][:], ACT.Relu).then_inc(v_ready, 1)

            def expert_step(i, q, up=True, mid=True, down=True, tail=True):
                if up:
                    rows_T(i + 1, 1 - q)
                if down:
                    hidden_T(i - 1, 1 - q)
                    deviation_h(i - 1, 1 - q)
                if tail:
                    deviation_y(i - 2, q)
                if mid:
                    hidden(i, q)
                if down:
                    relu_y(i - 1, 1 - q)

            rows_T(0, 0)
            expert_step(0, 0, down=False, tail=False)
            expert_step(1, 1, tail=False)
            with act.Fori(2, EXPERT_TILES - 3, 2) as i:
                expert_step(i, 0)
                expert_step(i + 1, 1)
            expert_step(EXPERT_TILES - 2, 0)
            expert_step(EXPERT_TILES - 1, 1, up=False)
            expert_step(EXPERT_TILES, 0, up=False, mid=False)
            expert_step(EXPERT_TILES + 1, 1, up=False, mid=False, down=False)

            nc.scalar.activation(gate[:, 0, :], lead[:], ACT.Sigmoid)
            nc.scalar.activation(gate[:, 1, :], lead[:], ACT.Sigmoid, scale=-1.0).then_inc(gate_ready, 1)
            act.wait_ge(gate_ready, 1)

            def gate_first(b, q, turn, first):
                act.wait_ge(y01_loaded[q], turn)
                if not first:
                    act.wait_ge(ysum_ready, b - 1)
                for j in range(J):
                    ins = nc.scalar.activation(y0g[q][:, j, :], y01[q][:, j, 0:D], ACT.Copy,
                                               scale=gate[:, 0, bass.ds(b * J + j, 1)])
                ins.then_inc(y0g_ready, 1)

            for q in range(2):
                gate_first(q, q, 16, True)
            with act.Fori(2, B - 1, 2) as b:
                for q in range(2):
                    gate_first(b + q, q, b * 8 + 16, False)

        @block.vector
        def _(dve):
            vec = nc.vector
            done = [0]

            def mark(ins):
                ins.then_inc(dve_setup, 1)
                done[0] += 1

            dve.wait_ge(pool_consts, 8)
            vec.tensor_scalar(ident[:], offs[:], 0.0, None, ALU.is_equal)
            vec.tensor_scalar(before[:], offs[:], 0.0, None, ALU.is_gt)
            vec.tensor_copy(iota_e[:], iota_ei[:])
            vec.tensor_scalar(base_e[:], iota_ei[:], float(REGION), None, ALU.mult)
            vec.tensor_copy(token[:], token_i[:])
            vec.tensor_copy(it_f[:], it_i[:])
            vec.memset(carry[:], 0.0)
            vec.memset(onesf[:], 1.0)
            vec.memset(ones_e[:], 1.0)
            vec.memset(eps[:], EPS)
            mark(vec.memset(padding[:], 0.0))
            dve.wait_ge(dve_setup, 1)
            mark(vec.memset(padding[:, D:D + 1], NOWHERE))
            assert done[0] == SETUP_PADDING
            for n in range(XL):
                dve.wait_ge(x_loaded[n], 16)
                for t in range(n * (NT // XL), (n + 1) * (NT // XL)):
                    ins = vec.bn_stats(st1[:, t, :], X[:, t, :])
            mark(ins)
            dve.wait_ge(dve_setup, 3)
            for t in range(NT):
                ins = vec.bn_aggr(mv1[:, t, :], st1[:, t, :])
            mark(ins)
            assert done[0] == SETUP_MV1
            dve.wait_ge(pe_setup, 1)
            mark(vec.tensor_copy(cT[:], bank[0][:, 0:B]))
            assert done[0] == SETUP_CT
            dve.wait_ge(pe_setup, 2)
            m = bank[1][:, 0:5 * B].rearrange("p (m b) -> p m b", m=5)
            vec.tensor_copy(mod[:, 0, :], m[:, 0, :])
            vec.tensor_scalar(mod[:, 1, :], m[:, 1, :], 1.0, None, ALU.add)
            vec.tensor_copy(mod[:, 3, :], m[:, 3, :])
            vec.tensor_scalar(mod[:, 4, :], m[:, 4, :], 1.0, None, ALU.add)
            vec.tensor_scalar(mod_sign[:], m[:, 2, :], 0.0, 2.0, ALU.is_ge, ALU.mult)
            mark(vec.tensor_scalar(gb_sign[:], bank[2][0:B, 0:D], 0.0, 2.0, ALU.is_ge, ALU.mult))
            dve.wait_ge(dve_setup, 6)
            vec.tensor_scalar(mod_sign[:], mod_sign[:], -1.0, None, ALU.add)
            mark(vec.tensor_scalar(gb_sign[:], gb_sign[:], -1.0, None, ALU.add))
            dve.wait_ge(dve_setup, 7)
            vec.tensor_tensor(mod_abs[:], mod_sign[:], m[:, 2, :], ALU.mult)
            mark(vec.tensor_tensor(gb_abs[:], gb_sign[:], bank[2][0:B, 0:D], ALU.mult))
            dve.wait_ge(dve_setup, 8)
            vec.scalar_tensor_tensor(mod[:, 2, :], mod_abs[:], 0.25, mod_sign[:], ALU.max, ALU.mult)
            mark(vec.scalar_tensor_tensor(gb_raw[:], gb_abs[:], 0.25, gb_sign[:], ALU.max, ALU.mult))
            assert done[0] == SETUP_GB
            dve.wait_ge(dve_setup, 9)
            dve.wait_ge(small_loaded, 16 * 9)
            vec.tensor_scalar(ga_bout[:], mod[:, 2, :], boutc[:], None, ALU.mult)
            dve.wait_ge(pe_setup, 3)
            mark(vec.tensor_tensor(cpT[:], bank[3][:, 0:CI * NS].rearrange("p (c s) -> p c s", c=CI), bp[:], ALU.mult))
            dve.wait_ge(dve_setup, 10)
            mark(vec.tensor_reduce(ccol[:], cpT[:], axis=AX, op=ALU.add))
            dve.wait_ge(dve_setup, 11)
            for ch in range(CI):
                vec.tensor_scalar(wz[:, ch, :], wout[:, ch, :], ccol[:, ch:ch + 1], None, ALU.mult)
                ins = vec.tensor_scalar(wu[:, ch, :], wout[:, ch, :], dcol[:, ch:ch + 1], None, ALU.mult)
            mark(ins)
            dve.wait_ge(act_setup, 2)
            mark(vec.reciprocal(rs1[:], sd1[:]))
            dve.wait_ge(dve_setup, 13)
            mark(vec.scalar_tensor_tensor(nm1[:], mv1[:, :, 0], -1.0, rs1[:], ALU.mult, ALU.mult))
            dve.wait_ge(pe_setup, 4)
            vec.tensor_copy(g1T[:], bank[4][:, 0:E * CF])
            mark(vec.tensor_copy(be1T[:], bank[4][:, E * CF:2 * E * CF]))
            assert done[0] == SETUP_B1
            dve.wait_ge(act_setup, 3)
            mark(vec.tensor_tensor(b1lo[:], b1f[:], b1hi[:], ALU.subtract))
            assert done[0] == SETUP_B1LO
            dve.wait_ge(rows_loaded, 48)
            dve.wait_ge(pe_setup, 5)
            per = E // 2
            for half in range(2):
                es = slice(half * per, (half + 1) * per)
                vec.tensor_tensor(c2[:, es, :], bank[1 + half][:].rearrange("p (e d) -> p e d", e=per),
                                  c2[:, es, :], ALU.add)
            mark(vec.tensor_tensor(W2[:], W2[:], g1T[:].rearrange("p (c o) -> p c o", o=1).broadcast_to([P, E * CF, D]),
                                   ALU.mult))
            assert done[0] == SETUP_W2G
            dve.wait_ge(pe_setup, 6)
            for half in range(2):
                w = W2[:, half * per * CF:(half + 1) * per * CF, :].rearrange("p (e c) d -> p e c d", c=CF)
                means = bank[5 + half][:].rearrange("p (e d) -> p e d", e=per)
                for ch in range(CF):
                    ins = vec.tensor_tensor(w[:, :, ch, :], w[:, :, ch, :], means, ALU.subtract)
            mark(ins)
            assert done[0] == SETUP_END

            def norm2(b, q):
                xb = X[:, tiles(b), :]
                dve.wait_ge(mix_done, b + 1)
                vec.tensor_tensor(xb, xb, bank[5][:].rearrange("p (j d) -> p j d", j=J), ALU.add).then_inc(x1_ready, 1)
                dve.wait_ge(x1_ready, b + 1)
                dve.nop(nofuse=True)
                for j in range(J):
                    ins = vec.bn_stats(st2[q][:, j, :], X[:, bass.ds(b * J + j, 1), :])
                ins.then_inc(st2_ready, 1)
                dve.wait_ge(st2_ready, b + 1)
                dve.nop(nofuse=True)
                for j in range(J):
                    ins = vec.bn_aggr(mv2[q][:, j, :], st2[q][:, j, :])
                ins.then_inc(mv2_ready, 1)
                dve.wait_ge(mv2_ready, b + 1)
                vec.tensor_scalar(ve2[q][:], mv2[q][:, :, 1], EPS, None, ALU.add).then_inc(ve2_ready, 1)

            def normalise2(b, q):
                dve.wait_ge(rs2_ready, b + 1)
                for j in range(J):
                    ins = vec.tensor_scalar(n2[q][:, j:j + 1, :], X[:, bass.ds(b * J + j, 1), :],
                                            mv2[q][:, j, 0:1], rs2[q][:, j:j + 1], ALU.subtract, ALU.mult)
                ins.then_inc(n2_ready, 1)

            def mix(b, q):
                dve.wait_ge(z_done, b + 1)
                vec.tensor_tensor_scan(scan[q][:], decay[:], bank[3][:], 0.0, ALU.mult, ALU.add).then_inc(scan_ready, 1)
                dve.wait_ge(skip_ready, b + 1)
                dve.wait_ge(scan_ready, b + 1)
                vec.scalar_tensor_tensor(mixT[q][:], scan[q][:], mod[:, 2, bass.ds(b, 1)], skip[q][:],
                                         ALU.mult, ALU.add).then_inc(mix_ready, 1)

            def route(b, q):
                dve.wait_ge(logit_done, b + 1)
                vec.tensor_tensor(logit[q][:], bank[7][:, 0:J * E].rearrange("p (j e) -> p j e", j=J),
                                  br[:].rearrange("p (o e) -> p o e", o=1).broadcast_to([P, J, E]),
                                  ALU.add).then_inc(logit_ready, 1)
                dve.wait_ge(logit_ready, b + 1)
                dve.nop(nofuse=True)
                for j in range(J):
                    ins = vec.max(best[q][:, j, :], logit[q][:, j, :])
                ins.then_inc(best_ready, 1)
                dve.wait_ge(best_ready, b + 1)
                dve.nop(nofuse=True)
                for j in range(J):
                    ins = vec.max_index(besti[q][:, j, :], best[q][:, j, :], logit[q][:, j, :])
                ins.then_inc(besti_ready, 1)
                dve.wait_ge(besti_ready, b + 1)
                vec.tensor_tensor(
                    hot[q][:], iota_e[:].rearrange("p (a b e) -> p a b e", a=1, b=1).broadcast_to([P, J, TOPK, E]),
                    besti[q][:, :, 0:TOPK].rearrange("p j (k o) -> p j k o", o=1).broadcast_to([P, J, TOPK, E]),
                    ALU.is_equal).then_inc(hot_ready, 1)
                dve.wait_ge(hot_ready, b + 1)
                vec.tensor_tensor(hots[q][:], hot[q][:, :, 0, :], hot[q][:, :, 1, :], ALU.add).then_inc(hots_ready, 1)
                vec.tensor_tensor(lead[:, tiles(b)], best[q][:, :, 0], best[q][:, :, 1], ALU.subtract)

            def assign(b, q, stored):
                if stored is not None:
                    dve.wait_ge(rows_stored[q], stored)
                vec.tensor_copy(rows[q][:, :, D], token[:, tiles(b)])
                vec.tensor_copy(rows[q][:, :, D + 1], besti[q][:, :, 0])
                dve.wait_ge(hots_ready, b + 1)
                vec.tensor_reduce(hotsum[q][:], hots[q][:].rearrange("p j e -> p e j"), axis=AX,
                                  op=ALU.add).then_inc(hotsum_ready, 1)
                dve.wait_ge(rank_done, b + 1)
                vec.tensor_tensor(place[q][:], bank[7][:, J * E:2 * J * E].rearrange("p (j e) -> p j e", j=J),
                                  base_e[:].rearrange("p (o e) -> p o e", o=1).broadcast_to([P, J, E]),
                                  ALU.add).then_inc(place_ready, 1)
                dve.wait_ge(hotsum_ready, b + 1)
                vec.tensor_tensor(carry[:], carry[:], hotsum[q][:], ALU.add).then_inc(carry_ready, 1)
                dve.wait_ge(place_ready, b + 1)
                vec.tensor_tensor(placed[q][:], hot[q][:],
                                  place[q][:].rearrange("p j (o e) -> p j o e", o=1).broadcast_to([P, J, TOPK, E]),
                                  ALU.mult).then_inc(placed_ready, 1)
                dve.wait_ge(placed_ready, b + 1)
                with nc.allow_low_precision(reason="one whole number below 2**24 and zeros"):
                    vec.tensor_reduce(slot[q][:], placed[q][:], axis=AX, op=ALU.add).then_inc(slot_ready, 1)

            def step(b, q, stored):
                norm2(b - 1, 1 - q)
                normalise2(b - 1, 1 - q)
                mix(b, q)
                route(b - 1, 1 - q)
                assign(b - 1, 1 - q, stored)

            per = 16 * J * TOPK
            mix(0, 0)
            step(1, 1, None)
            step(2, 0, None)
            with dve.Fori(3, B - 2, 2) as b:
                step(b, 1, (b - 1) * (per // 2))
                step(b + 1, 0, (b - 1) * (per // 2))
            step(B - 1, 1, (B - 2) // 2 * per)
            norm2(B - 1, 1)
            normalise2(B - 1, 1)
            route(B - 1, 1)
            assign(B - 1, 1, (B - 2) // 2 * per)

            ticks = [0]

            def link(ins):
                ins.then_inc(table_step, 1)
                ticks[0] += 1
                dve.wait_ge(table_step, ticks[0])

            dve.wait_ge(count_done, 1)
            vec.tensor_copy(cnt_i[:], bank[7][:, 0:E])
            link(vec.tensor_scalar(cnt[:], bank[7][:, 0:E], float(P - 1), None, ALU.add))
            link(vec.tensor_copy(nt_i[:], cnt[:]))
            link(vec.tensor_scalar(nt_i[:], nt_i[:], P.bit_length() - 1, None, ALU.logical_shift_right))
            link(vec.tensor_copy(nt_f[:], nt_i[:]))
            vec.tensor_scalar(jump[:], nt_f[:], -float(P), float(REGION), ALU.mult, ALU.add)
            link(vec.tensor_tensor_scan(ends[:], ones_e[:], nt_f[:], 0.0, ALU.mult, ALU.add))
            for e in range(E):
                vec.tensor_scalar(past[:, e, :], it_f[:], ends[:, e:e + 1], None, ALU.is_ge)
                ins = vec.tensor_scalar(hop[:, e, :], it_f[:], ends[:, e:e + 1], jump[:, e:e + 1], ALU.is_ge, ALU.mult)
            link(ins)
            vec.tensor_reduce(tile_e[:], past[:].rearrange("p e i -> p i e"), axis=AX, op=ALU.add)
            link(vec.tensor_reduce(tile_hop[:], hop[:].rearrange("p e i -> p i e"), axis=AX, op=ALU.add))
            vec.tensor_scalar(tile_ei[:], tile_e[:], float(E - 1), None, ALU.min)
            vec.scalar_tensor_tensor(tile_row[:], it_f[:], float(P), tile_hop[:], ALU.mult, ALU.add).then_inc(table_ready, 1)
            dve.wait_ge(table_ready, 1)

            def stats_h(i, q):
                dve.wait_ge(r_ready, i + 1)
                dve.nop(nofuse=True)
                vec.bn_stats(stf[q][:], r[q][:]).then_inc(stf_ready, 1)
                dve.wait_ge(stf_ready, i + 1)
                dve.nop(nofuse=True)
                vec.bn_aggr(mvf[q][:], stf[q][:]).then_inc(mvf_ready, 1)

            def stats_y(i, q):
                dve.wait_ge(v_ready, i + 1)
                dve.nop(nofuse=True)
                vec.bn_stats(sty[q][:], v[q][:]).then_inc(sty_ready, 1)
                dve.wait_ge(sty_ready, i + 1)
                dve.nop(nofuse=True)
                vec.bn_aggr(mvy[q][:], sty[q][:]).then_inc(mvy_ready, 1)

            def target_of(i, q):
                dve.wait_ge(hrow_loaded[q], (i + 2 - q) * 8)
                vec.scalar_tensor_tensor(targets[:, bass.ds(i, 1)], hrow[q][:, D + 1:D + 2], tile_e[:, bass.ds(i, 1)],
                                         hrow[q][:, D:D + 1], ALU.not_equal, ALU.add).then_inc(targets_ready, 1)

            def finish_y(i, q, first):
                e = dve.value_load(tile_ei[0:1, bass.ds(i, 1)], min_val=0, max_val=E - 1)
                dve.wait_ge(sdy_ready, i + 1)
                vec.reciprocal(rsy[q][:], sdy[q][:]).then_inc(rsy_ready, 1)
                vec.scalar_tensor_tensor(vg[q][:].rearrange("p (o d) -> p o d", o=1), v[q][:].rearrange("p (o d) -> p o d", o=1),
                                         mvy[q][:, 0:1], g2[:, bass.ds(e, 1), :], ALU.subtract, ALU.mult).then_inc(vg_ready, 1)
                if not first:
                    dve.wait_ge(results_stored[q], (i - q) * 8)
                dve.wait_ge(rsy_ready, i + 1)
                dve.wait_ge(vg_ready, i + 1)
                vec.scalar_tensor_tensor(y[q][:].rearrange("p (o d) -> p o d", o=1), vg[q][:].rearrange("p (o d) -> p o d", o=1),
                                         rsy[q][:], be2[:, bass.ds(e, 1), :], ALU.mult, ALU.add).then_inc(y_ready, 1)

            def scale_y(i, q):
                e = dve.value_load(tile_ei[0:1, bass.ds(i, 1)], min_val=0, max_val=E - 1)
                dve.wait_ge(sdf_ready, i + 1)
                vec.reciprocal(rsf[q][:], sdf[q][:]).then_inc(rsf_ready, 1)
                dve.wait_ge(y_done, i + 1)
                dve.wait_ge(rsf_ready, i + 1)
                vec.scalar_tensor_tensor(v0[q][:].rearrange("p (o d) -> p o d", o=1),
                                         bank[4 + q][:, 0:D].rearrange("p (o d) -> p o d", o=1),
                                         rsf[q][:], c2[:, bass.ds(e, 1), :], ALU.mult, ALU.add).then_inc(v0_ready, 1)

            def expert_step(i, q, up=True, down=True, tail=True, first=False):
                if up:
                    target_of(i + 1, 1 - q)
                if down:
                    stats_h(i - 1, 1 - q)
                if tail:
                    stats_y(i - 2, q)
                    finish_y(i - 2, q, first)
                if down:
                    scale_y(i - 1, 1 - q)

            target_of(0, 0)
            target_of(1, 1)
            expert_step(1, 1, tail=False)
            expert_step(2, 0, first=True)
            expert_step(3, 1, first=True)
            with dve.Fori(4, EXPERT_TILES - 3, 2) as i:
                expert_step(i, 0)
                expert_step(i + 1, 1)
            expert_step(EXPERT_TILES - 2, 0)
            expert_step(EXPERT_TILES - 1, 1, up=False)
            expert_step(EXPERT_TILES, 0, up=False)
            expert_step(EXPERT_TILES + 1, 1, up=False, down=False)

            dve.wait_ge(gate_ready, 1)
            dve.wait_ge(gb_loaded, 16)

            def sums(b, q, stored):
                dve.wait_ge(y0g_ready, b + 1)
                for j in range(J):
                    ins = vec.scalar_tensor_tensor(ysum[q][:, j, :], y01[q][:, j, D:2 * D], gate[:, 1, bass.ds(b * J + j, 1)],
                                                   y0g[q][:, j, :], ALU.mult, ALU.add)
                ins.then_inc(ysum_ready, 1)
                dve.wait_ge(ysum_ready, b + 1)
                vec.tensor_tensor(ygb[q][:], ysum[q][:], gb_rows[:, bass.ds(b, 1), :].broadcast_to([P, J, D]),
                                  ALU.mult).then_inc(ygb_ready, 1)
                dve.wait_ge(ygb_ready, b + 1)
                if stored is not None:
                    dve.wait_ge(out_stored[q], stored)
                vec.tensor_tensor(o[q][:], ygb[q][:], X[:, tiles(b), :], ALU.add).then_inc(o_ready, 1)

            for q in range(2):
                sums(q, q, None)
            with dve.Fori(2, B - 1, 2) as b:
                for q in range(2):
                    sums(b + q, q, b * 8)

        @block.tensor
        def _(pe):
            mm, tr = nc.tensor.matmul, nc.tensor.transpose
            pe.wait_ge(dve_setup, SETUP_PADDING)
            pe.wait_ge(act_setup, 1)
            tr(bank[0][:, 0:B], c_act[:], ident[0:B, 0:B]).then_inc(pe_setup, 1)
            pe.wait_ge(dve_setup, SETUP_CT)
            for n in range(5):
                mm(bank[1][:, n * B:(n + 1) * B], wmod[:, n * D:(n + 1) * D], cT[:], start=True, stop=True)
            mm(bank[2][0:B, 0:D], cT[:], wmod[:, 5 * D:6 * D], start=True, stop=True).then_inc(pe_setup, 1)
            pe.wait_ge(small_loaded, 16 * 9)
            for ch in range(CI):
                ins = tr(bank[3][:, ch * NS:(ch + 1) * NS], cp[:, ch * P:(ch + 1) * P], ident[0:NS, 0:NS])
            ins.then_inc(pe_setup, 1)
            pe.wait_ge(w2_loaded, 64)
            tr(bank[4][:, 0:E * CF], g1r[:], ident[0:E * CF, 0:E * CF])
            tr(bank[4][:, E * CF:2 * E * CF], be1r[:], ident[0:E * CF, 0:E * CF]).then_inc(pe_setup, 1)
            pe.wait_ge(dve_setup, SETUP_B1)
            per = E // 2
            for e in range(E):
                for ch in range(CF):
                    n = e * CF + ch
                    ins = mm(bank[1 + e // per][:, (e % per) * D:(e % per + 1) * D], be1T[:, n:n + 1].broadcast_to([P, P]),
                             W2[:, n, :], start=(ch == 0), stop=(ch == CF - 1))
            ins.then_inc(pe_setup, 1)
            pe.wait_ge(dve_setup, SETUP_W2G)
            for half in range(2):
                w = W2[:, half * per * CF:(half + 1) * per * CF, :].rearrange("p (e c) d -> p e c d", c=CF)
                for ch in range(CF):
                    ins = mm(bank[5 + half][:].rearrange("p (e d) -> p e d", e=per), mean_w[:], w[:, :, ch, :],
                             start=(ch == 0), stop=(ch == CF - 1))
            ins.then_inc(pe_setup, 1)
            pe.wait_ge(dve_setup, SETUP_END)

            def up(b, q):
                pe.wait_ge(n1_ready, b + 1)
                for j in range(J):
                    ins = tr(bank[0][:, j * P:(j + 1) * P], n1[q][:, j, :], ident[:])
                ins.then_inc(t1_done, 1)
                pe.wait_ge(h1T_ready, b + 1)
                mm(bank[1][:], win[:, 0:P], h1T[q][:], start=True, stop=True).then_inc(xi0_done, 1)
                mm(bank[2][:], win[:, P:2 * P], h1T[q][:], start=True, stop=True).then_inc(xi1_done, 1)

            def down(b, q):
                pe.wait_ge(xi0_ready, b + 1)
                mm(bank[3][:], wz[:, 0, :], xi[q][:, 0, :], start=True, stop=False)
                mm(bank[4][:], wu[:, 0, :], xi[q][:, 0, :], start=True, stop=False)
                pe.wait_ge(xi1_ready, b + 1)
                mm(bank[3][:], wz[:, 1, :], xi[q][:, 1, :], start=False, stop=True).then_inc(z_done, 1)
                mm(bank[4][:], wu[:, 1, :], xi[q][:, 1, :], start=False, stop=True).then_inc(u_done, 1)

            def mixed(b, q):
                pe.wait_ge(mix_ready, b + 1)
                for j in range(J):
                    ins = tr(bank[5][:, j * P:(j + 1) * P], mixT[q][:, j * P:(j + 1) * P], ident[:])
                ins.then_inc(mix_done, 1)

            def norm2_T(b, q, first=False):
                pe.wait_ge(n2_ready, b + 1)
                if not first:
                    pe.wait_ge(rows_ready, b)
                for j in range(J):
                    ins = tr(bank[6][:, j * P:(j + 1) * P], n2[q][:, j, :], ident[:])
                ins.then_inc(t2_done, 1)

            def logits(b, q, first=False):
                pe.wait_ge(h2T_ready, b + 1)
                for j in range(J):
                    ins = tr(bank[6][:, j * P:(j + 1) * P], h2T[q][:, j * P:(j + 1) * P], ident[:])
                ins.then_inc(back_done, 1)
                if not first:
                    pe.wait_ge(place_ready, b)
                for j in range(J):
                    ins = mm(bank[7][:, j * E:(j + 1) * E], h2T[q][:, j * P:(j + 1) * P], wr[:], start=True, stop=True)
                ins.then_inc(logit_done, 1)

            def rank(b, q, first=False):
                acc = bank[7][:, J * E:2 * J * E].rearrange("p (j e) -> p j e", j=J)
                pe.wait_ge(hots_ready, b + 1)
                mm(acc, before[:], hots[q][:], start=True, stop=False)
                for j in range(J - 1):
                    mm(acc[:, j + 1:J, :], ones[:], hots[q][:, j:j + 1, :].broadcast_to([P, J - 1 - j, E]),
                       start=False, stop=False)
                if not first:
                    pe.wait_ge(carry_ready, b)
                mm(acc, ones[:], carry[:].rearrange("p (o e) -> p o e", o=1).broadcast_to([P, J, E]),
                   start=False, stop=True).then_inc(rank_done, 1)

            def step(b, q, first=False):
                up(b, q)
                norm2_T(b - 1, 1 - q, first)
                down(b, q)
                logits(b - 1, 1 - q, first)
                mixed(b, q)
                rank(b - 1, 1 - q, first)

            up(0, 0)
            down(0, 0)
            mixed(0, 0)
            step(1, 1, first=True)
            with pe.Fori(2, B - 1, 2) as b:
                step(b, 0)
                step(b + 1, 1)
            norm2_T(B - 1, 1)
            logits(B - 1, 1)
            rank(B - 1, 1)
            pe.wait_ge(carry_ready, B)
            pe.wait_ge(place_ready, B)
            mm(bank[7][:, 0:E], ones[:], carry[:], start=True, stop=True).then_inc(count_done, 1)

            pe.wait_ge(w1_loaded, 16)
            pe.wait_ge(b1_stored, 32)
            pe.wait_ge(table_ready, 1)

            def rows_T(i, q, first=False):
                pe.wait_ge(hrow_loaded[q], (i + 2 - q) * 8)
                if not first:
                    pe.wait_ge(h3T_ready, i)
                tr(bank[0][:, 0:P], hrow[q][:, 0:D], ident[:]).then_inc(t3_done, 1)

            def hidden(i, q):
                e = pe.value_load(tile_ei[0:1, bass.ds(i, 1)], min_val=0, max_val=E - 1)
                h = bank[1 + q][:].rearrange("p (o f) -> p o f", o=1)
                pe.wait_ge(h3T_ready, i + 1)
                mm(h, onesr[:], b1_parts[:, bass.ds(e, 1), :], start=True, stop=False)
                mm(h, h3T[q][:], W1[:, bass.ds(e, 1), :], start=False, stop=True).then_inc(h_done, 1)

            def hidden_T(i, q):
                pe.wait_ge(r_ready, i + 1)
                for ch in range(CF):
                    ins = tr(bank[3][:, ch * P:(ch + 1) * P], r[q][:, ch * P:(ch + 1) * P], ident[:])
                ins.then_inc(tr_done, 1)

            def down_y(i, q, first=False):
                e = pe.value_load(tile_ei[0:1, bass.ds(i, 1)], min_val=0, max_val=E - 1)
                acc = bank[4 + q][:, 0:D].rearrange("p (o d) -> p o d", o=1)
                pe.wait_ge(rT_ready, i + 1)
                if not first:
                    pe.wait_ge(v0_ready, i - 1)
                for ch in range(CF):
                    ins = mm(acc, rT[q][:, ch * P:(ch + 1) * P], W2[:, bass.ds(e * CF + ch, 1), :],
                             start=(ch == 0), stop=(ch == CF - 1))
                ins.then_inc(y_done, 1)

            def expert_step(i, q, upper=True, mid=True, lower=True, first=False):
                if upper:
                    rows_T(i + 1, 1 - q)
                if lower:
                    hidden_T(i - 1, 1 - q)
                if mid:
                    hidden(i, q)
                if lower:
                    down_y(i - 1, 1 - q, first)

            rows_T(0, 0, first=True)
            expert_step(0, 0, lower=False)
            expert_step(1, 1, first=True)
            expert_step(2, 0, first=True)
            expert_step(3, 1)
            with pe.Fori(4, EXPERT_TILES - 3, 2) as i:
                expert_step(i, 0)
                expert_step(i + 1, 1)
            expert_step(EXPERT_TILES - 2, 0)
            expert_step(EXPERT_TILES - 1, 1, upper=False)
            expert_step(EXPERT_TILES, 0, upper=False, mid=False)


SETUP_PADDING, SETUP_MV1, SETUP_CT, SETUP_GB, SETUP_B1, SETUP_B1LO, SETUP_W2G, SETUP_END = 2, 4, 5, 9, 15, 16, 17, 18

_INS = ['L0_attn_x', 'L0_attn_Win', 'L0_attn_bin_', 'L0_attn_Bp', 'L0_attn_Cp', 'L0_attn_Dp', 'L0_attn_Wout',
        'L0_attn_bout', 'L0_ffn_Wr', 'L0_ffn_br', 'L0_ffn_W1', 'L0_ffn_b1', 'L0_ffn_g1', 'L0_ffn_be1', 'L0_ffn_W2',
        'L0_ffn_b2', 'L0_ffn_g2', 'L0_ffn_be2', 'L0_c', 'L0_wmod']


def kernel(**inputs):
    import numpy as _np
    import concourse.bacc as _bacc
    from concourse.bass_utils import run_bass_kernel_spmd as _run

    nc = _bacc.Bacc("TRN2", target_bir_lowering=False, num_devices=1)
    arrays, args = {}, []
    for name in _INS:
        a = _np.ascontiguousarray(inputs[name])
        arrays[f"in_{name}"] = a
        args.append(nc.dram_tensor(f"in_{name}", a.shape, mybir.dt.from_np(a.dtype), kind="ExternalInput").ap())
    shape = tuple(inputs['L0_attn_x'].shape)
    args.append(nc.dram_tensor("out_x", shape, mybir.dt.float32, kind="ExternalOutput").ap())
    adaln_ssm_moe_kernel(nc, *args)
    r = _run(nc, [arrays], core_ids=[0])
    return r.results[0]["out_x"]
```

```python
from contextlib import ExitStack

import concourse.bass as bass
from concourse import mybir


def adaln_ssm_moe_kernel(nc, x_in, win_in, bin_in, bp_in, cp_in, dp_in, wout_in, bout_in, wr_in, br_in,
                         w1_in, b1_in, g1_in, be1_in, w2_in, b2_in, g2_in, be2_in, c_in, wmod_in, out):
    F32, F32R, BF16 = mybir.dt.float32, mybir.dt.float32r, mybir.dt.bfloat16
    I32, U32 = mybir.dt.int32, mybir.dt.uint32
    ALU = mybir.AluOpType
    ACT = mybir.ActivationFunctionType
    AX = mybir.AxisListType.X

    B, L, D = x_in.shape
    P = 128
    J = L // P
    T = B * L
    NT = T // P
    DI, NS = bp_in.shape
    CI = DI // P
    E, _, F = w1_in.shape
    CF = F // P
    TOPK = 2
    EPS = 1e-5
    DECAY = 0.9
    REGION = T + P
    EXPERT_TILES = TOPK * NT + E
    SPARE = E * REGION
    NSPARE = EXPERT_TILES - TOPK * NT
    ROW = D + 2
    NOWHERE = 65536.0
    assert D == P and EXPERT_TILES % 2 == 0 and B % 2 == 0

    x_v = x_in.rearrange("b l d -> (b l) d").rearrange("(n p) d -> p n d", p=P)
    out_v = out.rearrange("b l d -> (b l) d").rearrange("(n p) d -> p n d", p=P)
    rows_d = nc.dram_tensor("expert_rows", (SPARE + NSPARE * P, ROW), F32, kind="Internal").ap()
    results_d = nc.dram_tensor("expert_results", (TOPK * T, D), F32, kind="Internal").ap()
    results_v = results_d.rearrange("(n p k) d -> p n (k d)", p=P, k=TOPK)
    gates_d = nc.dram_tensor("gate_b_rows", (1, B * D), F32, kind="Internal").ap()

    with ExitStack() as ctx:
        def sb(name, shape, dt=F32):
            return ctx.enter_context(nc.sbuf_tensor(name, shape, dt))

        def sem(name):
            return ctx.enter_context(nc.semaphore(name))

        bank = [ctx.enter_context(nc.psum_tensor(f"bank{n}", [P, 512], F32)) for n in range(8)]

        X = sb("X", [P, NT, D])
        W1 = sb("W1", [P, E, F])
        W2 = sb("W2", [P, E * CF, D])
        c2 = sb("c2", [P, E, D])
        g2 = sb("g2", [P, E, D])
        be2 = sb("be2", [P, E, D])
        gb_rows = sb("gb_rows", [P, B, D])
        win = sb("win", [P, DI])
        wout = sb("wout", [P, CI, D])
        wz = sb("wz", [P, CI, D])
        wu = sb("wu", [P, CI, D])
        wr = sb("wr", [P, E])
        br = sb("br", [P, E])
        wmod = sb("wmod", [P, 6 * D])
        bcol = sb("bcol", [P, CI])
        dcol = sb("dcol", [P, CI])
        boutc = sb("boutc", [P, 1])
        bp = sb("bp", [P, CI, NS])
        cp = sb("cp", [NS, DI])
        cpT = sb("cpT", [P, CI, NS])
        ccol = sb("ccol", [P, CI])
        c_sb = sb("c_sb", [B, D])
        c_act = sb("c_act", [B, D])
        cT = sb("cT", [P, B])
        mod = sb("mod", [P, 5, B])
        mod_sign = sb("mod_sign", [P, B])
        mod_abs = sb("mod_abs", [P, B])
        ga_bout = sb("ga_bout", [P, B])
        gb_raw = sb("gb_raw", [B, D])
        gb_sign = sb("gb_sign", [B, D])
        gb_abs = sb("gb_abs", [B, D])
        g1r = sb("g1r", [E * CF, P])
        be1r = sb("be1r", [E * CF, P])
        g1T = sb("g1T", [P, E * CF])
        g1m = sb("g1m", [P, E * CF])
        be1T = sb("be1T", [P, E * CF])
        spread = [sb(f"spread_{q}", [P, CF, P]) for q in range(2)]
        b1f = sb("b1f", [E, F])
        b1hi = sb("b1hi", [E, F], F32R)
        b1lo = sb("b1lo", [E, F], F32R)
        b1_parts = sb("b1_parts", [2, E, F], F32R)
        onesr = sb("onesr", [2, P], F32R)
        onesf = sb("onesf", [2, P])
        offs = sb("offs", [P, P], I32)
        ident = sb("ident", [P, P])
        before = sb("before", [P, P], BF16)
        ones = sb("ones", [P, P], BF16)
        decay = sb("decay", [P, L])
        eps = sb("eps", [P, 1])
        iota_e = sb("iota_e", [P, E])
        iota_ei = sb("iota_ei", [P, E], I32)
        base_e = sb("base_e", [P, E])
        token_i = sb("token_i", [P, NT], I32)
        token = sb("token", [P, NT])
        padding = sb("padding", [P, ROW])
        lead = sb("lead", [P, NT])
        n1 = [sb(f"n1_{q}", [P, J, D]) for q in range(2)]
        h1T = [sb(f"h1T_{q}", [P, L]) for q in range(2)]
        xi = [sb(f"xi_{q}", [P, CI, L]) for q in range(2)]
        scan = [sb(f"scan_{q}", [P, L]) for q in range(2)]
        skip = [sb(f"skip_{q}", [P, L]) for q in range(2)]
        mixT = [sb(f"mixT_{q}", [P, L]) for q in range(2)]
        st = [sb(f"st_{q}", [P, 2 * J, 6]) for q in range(2)]
        mv = [sb(f"mv_{q}", [P, 2 * J, 2]) for q in range(2)]
        ve = [sb(f"ve_{q}", [P, 2 * J]) for q in range(2)]
        sq = [sb(f"sq_{q}", [P, 2 * J]) for q in range(2)]
        hv = [sb(f"hv_{q}", [P, 2 * J]) for q in range(2)]
        rs = [sb(f"rs_{q}", [P, 2 * J]) for q in range(2)]
        nm = [sb(f"nm_{q}", [P, 2 * J]) for q in range(2)]
        n2 = [sb(f"n2_{q}", [P, J, D]) for q in range(2)]
        h2T = [sb(f"h2T_{q}", [P, L]) for q in range(2)]
        rows = [sb(f"rows_{q}", [P, J, ROW]) for q in range(2)]
        logit = [sb(f"logit_{q}", [P, J, E]) for q in range(2)]
        best = [sb(f"best_{q}", [P, J, 8]) for q in range(2)]
        besti = [sb(f"besti_{q}", [P, J, 8], U32) for q in range(2)]
        hot = [sb(f"hot_{q}", [P, J, TOPK, E]) for q in range(2)]
        hots = [sb(f"hots_{q}", [P, J, E], BF16) for q in range(2)]
        hotsum = [sb(f"hotsum_{q}", [P, E]) for q in range(2)]
        carry = sb("carry", [P, E], BF16)
        place = [sb(f"place_{q}", [P, J, E]) for q in range(2)]
        placed = [sb(f"placed_{q}", [P, J, TOPK, E]) for q in range(2)]
        slot = [sb(f"slot_{q}", [P, J, TOPK], I32) for q in range(2)]
        cnt = sb("cnt", [P, E])
        cnt_i = sb("cnt_i", [P, E], I32)
        nt_i = sb("nt_i", [P, E], I32)
        nt_f = sb("nt_f", [P, E])
        ends = sb("ends", [P, E])
        ones_e = sb("ones_e", [P, E])
        jump = sb("jump", [P, E])
        it_i = sb("it_i", [P, EXPERT_TILES], I32)
        it_f = sb("it_f", [P, EXPERT_TILES])
        past = sb("past", [P, E, EXPERT_TILES])
        hop = sb("hop", [P, E, EXPERT_TILES])
        tile_e = sb("tile_e", [P, EXPERT_TILES])
        tile_hop = sb("tile_hop", [P, EXPERT_TILES])
        tile_ei = sb("tile_ei", [P, EXPERT_TILES], I32)
        tile_row = sb("tile_row", [P, EXPERT_TILES], I32)
        hrow = [sb(f"hrow_{q}", [P, ROW]) for q in range(2)]
        h3T = [sb(f"h3T_{q}", [P, P]) for q in range(2)]
        r = h1T
        rT = h2T
        stf = [sb(f"stf_{q}", [P, 6]) for q in range(2)]
        mve = [sb(f"mve_{q}", [P, 2, 2]) for q in range(2)]
        sde = [sb(f"sde_{q}", [P, 2]) for q in range(2)]
        rse = [sb(f"rse_{q}", [P, 2]) for q in range(2)]
        v0 = [sb(f"v0_{q}", [P, D]) for q in range(2)]
        v = [sb(f"v_{q}", [P, D]) for q in range(2)]
        sty = [sb(f"sty_{q}", [P, 6]) for q in range(2)]
        vg = [sb(f"vg_{q}", [P, D]) for q in range(2)]
        y = [sb(f"y_{q}", [P, D]) for q in range(2)]
        targets = sb("targets", [P, EXPERT_TILES], I32)
        target = [sb(f"target_{q}", [P, 1], I32) for q in range(2)]
        gate = sb("gate", [P, TOPK, NT])
        SLOTS = 4
        y01 = [W1[:, :, :].rearrange("p e f -> p (e f)")[:, n * J * TOPK * D:(n + 1) * J * TOPK * D].rearrange(
            "p (j k) -> p j k", j=J) for n in range(SLOTS)]
        y0g = n1
        ysum = n2
        ygb = [t[:, :].rearrange("p (j d) -> p j d", j=J) for t in scan]

        XL = B // 2
        x_loaded = [sem(f"x_loaded{n}") for n in range(XL)]
        small_loaded = sem("small_loaded")
        mod_loaded = sem("mod_loaded")
        w1_loaded, w2_loaded, gains_loaded, rows_loaded = (
            sem("w1_loaded"), sem("w2_loaded"), sem("gains_loaded"), sem("rows_loaded"))
        b2_loaded = sem("b2_loaded")
        spare_stored = sem("spare_stored")
        pool_consts = sem("pool_consts")
        dve_setup, act_setup, pe_setup = sem("dve_setup"), sem("act_setup"), sem("pe_setup")
        gb_stored, gb_loaded, b1_stored = sem("gb_stored"), sem("gb_loaded"), sem("b1_stored")
        (n1_ready, t1_done, h1T_ready, xi0_done, xi1_done, xi0_ready, xi1_ready, z_done, u_done, skip_ready,
         scan_ready, mix_ready, mix_done) = [sem(n) for n in (
             "n1_ready", "t1_done", "h1T_ready", "xi0_done", "xi1_done", "xi0_ready", "xi1_ready", "z_done",
             "u_done", "skip_ready", "scan_ready", "mix_ready", "mix_done")]
        (x1_ready, n2_ready, t2_done, h2T_ready, back_done, logit_done, rows_ready, logit_ready, best_ready,
         besti_ready, hot_ready, hots_ready, carry_ready, rank_done, place_ready, placed_ready, slot_ready,
         hotsum_ready, ids_ready) = [sem(n) for n in (
             "x1_ready", "n2_ready", "t2_done", "h2T_ready", "back_done", "logit_done", "rows_ready", "logit_ready",
             "best_ready", "besti_ready", "hot_ready", "hots_ready", "carry_ready", "rank_done", "place_ready",
             "placed_ready", "slot_ready", "hotsum_ready", "ids_ready")]
        stats_ready, mv_ready, ve_ready, guess_ready, nm_ready = [sem(n) for n in (
            "stats_ready", "mv_ready", "ve_ready", "guess_ready", "nm_ready")]
        newton = [[sem(f"{what}{n}_ready") for what in ("sq", "hv", "rs")] for n in range(3)]
        spread_ready = sem("spread_ready")
        bias_done, means_done, c2_ready, w2_ready = sem("bias_done"), sem("means_done"), sem("c2_ready"), sem("w2_ready")
        rows_stored = [sem(f"rows_stored{q}") for q in range(2)]
        count_done, table_step, table_ready, padding_stored = (
            sem("count_done"), sem("table_step"), sem("table_ready"), sem("padding_stored"))
        hrow_loaded = [sem(f"hrow_loaded{q}") for q in range(2)]
        (t3_done, h3T_ready, h_done, r_ready, tr_done, rT_ready, y_done, stf_ready, v0_ready, v_ready, sty_ready,
         vg_ready, y_ready, targets_ready, target_ready) = [sem(n) for n in (
             "t3_done", "h3T_ready", "h_done", "r_ready", "tr_done", "rT_ready", "y_done", "stf_ready", "v0_ready",
             "v_ready", "sty_ready", "vg_ready", "y_ready", "targets_ready", "target_ready")]
        mve_ready, sde_ready, rse_ready = sem("mve_ready"), sem("sde_ready"), sem("rse_ready")
        results_stored = [sem(f"results_stored{q}") for q in range(2)]
        gate_ready = sem("gate_ready")
        y01_loaded = [sem(f"y01_loaded{n}") for n in range(SLOTS)]
        y0g_ready, ysum_ready, ygb_ready, o_ready = (
            sem("y0g_ready"), sem("ysum_ready"), sem("ygb_ready"), sem("o_ready"))
        out_stored = sem("out_stored")

        block = ctx.enter_context(nc.Block())

        HALF = EXPERT_TILES // 2
        PER = 16 * J * TOPK

        def on(i, n):
            return not isinstance(i, int) or 0 <= i < n

        FIRST1, LOOP1, LAST1 = -2, (6, B - 2), B + 2
        FIRST2, LOOP2, LAST2 = -1, (8, EXPERT_TILES - 2), EXPERT_TILES + 4
        assert B % 2 == 0 and E == B // 2

        def norms(s):
            return slice(0 if on(s - 1, EXPERT_TILES) else 1, 2 if on(s - 4, EXPERT_TILES) else 1)

        def run(engine, step, first, loop, last):
            for s in range(first, loop[0]):
                step(s, s % 2, s // 2)
            with engine.Fori(loop[0] // 2, loop[1] // 2) as pair:
                step(pair * 2, 0, pair)
                step(pair * 2 + 1, 1, pair)
            for s in range(loop[1], last + 1):
                step(s, s % 2, s // 2)

        def run_tiles(name, engine, step, oldest):
            def one(s):
                return lambda k: engine.value_load(tile_ei[0:1, bass.ds(s + k, 1)], min_val=0, max_val=E - 1)

            for s in range(FIRST2, LOOP2[0]):
                step(s, s % 2, one(s))
            with engine.Fori(LOOP2[0] // 2, LOOP2[1] // 2) as pair:
                _, four = nc.values_load_multi_w_load_instructions(
                    tile_ei[0:1, bass.ds(pair * 2 + oldest, 4)], engines=(name,), min_val=0, max_val=E - 1,
                    skip_runtime_bounds_check_because="tile_ei is a count of experts, cut off at E - 1")
                step(pair * 2, 0, lambda k: four[k - oldest])
                step(pair * 2 + 1, 1, lambda k: four[k - oldest + 1])
            for s in range(LOOP2[1], LAST2 + 1):
                step(s, s % 2, one(s))

        def tiles(b):
            return bass.ds(b * J, J)

        @block.sync
        def _(sp):
            sp.dma_start(c_sb[:], c_in).then_inc(mod_loaded, 16)
            sp.dma_start(wmod[:], wmod_in).then_inc(mod_loaded, 16)
            NX = NT // XL
            sp.dma_start(X[:, 0:NX, :], x_v[:, 0:NX, :]).then_inc(x_loaded[0], 16)
            sp.dma_start(win[:], win_in).then_inc(small_loaded, 16)
            sp.dma_start(wout[:], wout_in.rearrange("(c p) d -> p c d", p=P)).then_inc(small_loaded, 16)
            sp.dma_start(bp[:], bp_in.rearrange("(c p) s -> p c s", p=P)).then_inc(small_loaded, 16)
            sp.dma_start(cp[:], cp_in).then_inc(small_loaded, 16)
            sp.dma_start(bcol[:], bin_in.rearrange("(c p) -> p c", p=P), allow_slow_non_contiguous=True).then_inc(small_loaded, 16)
            sp.dma_start(dcol[:], dp_in.rearrange("(c p) -> p c", p=P), allow_slow_non_contiguous=True).then_inc(small_loaded, 16)
            sp.dma_start(boutc[:], bout_in.rearrange("(p o) -> p o", o=1), allow_slow_non_contiguous=True).then_inc(small_loaded, 16)
            sp.dma_start(wr[:], wr_in).then_inc(small_loaded, 16)
            sp.dma_start(br[:], br_in.rearrange("(o e) -> o e", o=1).broadcast_to([P, E])).then_inc(small_loaded, 16)
            sp.dma_start(g1r[:], g1_in.rearrange("e (c p) -> (e c) p", p=P)).then_inc(gains_loaded, 16)
            sp.dma_start(be1r[:], be1_in.rearrange("e (c p) -> (e c) p", p=P)).then_inc(gains_loaded, 16)
            sp.dma_start(b1f[:], b1_in).then_inc(gains_loaded, 16)
            sp.dma_start(X[:, NX:2 * NX, :], x_v[:, NX:2 * NX, :]).then_inc(x_loaded[1], 16)

            def on_every_partition(src):
                return src.rearrange("(o e) d -> o e d", o=1).broadcast_to([P, E, D])

            sp.dma_start(c2[:], on_every_partition(b2_in)).then_inc(b2_loaded, 16)
            sp.dma_start(W2[:], w2_in.rearrange("e (c p) d -> p (e c) d", p=P)).then_inc(w2_loaded, 16)
            for n in range(2, XL):
                sp.dma_start(X[:, n * NX:(n + 1) * NX, :], x_v[:, n * NX:(n + 1) * NX, :]).then_inc(x_loaded[n], 16)
            sp.dma_start(g2[:], on_every_partition(g2_in)).then_inc(rows_loaded, 16)
            sp.dma_start(be2[:], on_every_partition(be2_in)).then_inc(rows_loaded, 16)
            sp.dma_start(W1[:], w1_in.rearrange("e p f -> p e f")).then_inc(w1_loaded, 16)
            sp.wait_ge(dve_setup, SETUP_GB)
            sp.dma_start(gates_d.rearrange("o (b d) -> (o b) d", b=B), gb_raw[:]).then_inc(gb_stored, 16)
            sp.wait_ge(gb_stored, 16)
            sp.dma_start(gb_rows[:], gates_d.rearrange("o (b d) -> o b d", b=B).broadcast_to([P, B, D])).then_inc(gb_loaded, 16)
            sp.wait_ge(dve_setup, SETUP_END)
            sp.wait_ge(act_setup, 2)
            sp.dma_start(b1_parts[0:1, :, :].bitcast(F32), b1hi[:].bitcast(F32)).then_inc(b1_stored, 16)
            sp.dma_start(b1_parts[1:2, :, :].bitcast(F32), b1lo[:].bitcast(F32)).then_inc(b1_stored, 16)
            sp.wait_ge(dve_setup, SETUP_PADDING)
            for n in range(NSPARE):
                sp.dma_start(rows_d[SPARE + n * P:SPARE + (n + 1) * P, :], padding[:]).then_inc(spare_stored, 16)
            sp.wait_ge(table_step, 1)
            for e in range(E):
                n = sp.value_load(cnt_i[0:1, e:e + 1], min_val=0, max_val=T)
                sp.dma_start(rows_d[bass.ds(n + e * REGION, P), :], padding[:]).then_inc(padding_stored, 16)
            sp.wait_ge(table_ready, 1)
            sp.wait_ge(spare_stored, 16 * NSPARE)
            sp.wait_ge(padding_stored, 16 * E)
            for q in range(2):
                sp.wait_ge(rows_stored[q], 16 * J * TOPK * (B // 2))

            def load_rows(i, q, first):
                start = sp.value_load(tile_row[0:1, bass.ds(i, 1)], min_val=0, max_val=SPARE + (NSPARE - 1) * P)
                if not first:
                    sp.wait_ge(t3_done, i - 1)
                    sp.wait_ge(targets_ready, i - 1)
                sp.dma_start(hrow[q][:], rows_d[bass.ds(start, P), :]).then_inc(hrow_loaded[q], 16)

            for q in range(2):
                load_rows(q, q, True)
            with sp.Fori(2, EXPERT_TILES - 1, 2) as i:
                for q in range(2):
                    load_rows(i + q, q, False)
            for q in range(2):
                sp.wait_ge(results_stored[q], 16 * HALF)

            def load_results(b, n):
                sp.dma_start(y01[n], results_v[:, tiles(b), :]).then_inc(y01_loaded[n], 16)

            def store_out(b):
                sp.wait_ge(o_ready, b + 1)
                sp.dma_start(out_v[:, tiles(b), :], X[:, tiles(b), :]).then_inc(out_stored, 16)

            for n in range(SLOTS):
                load_results(n, n)
            with sp.Fori(1, B // SLOTS) as turn:
                for n in range(SLOTS):
                    b = turn * SLOTS + n
                    sp.wait_ge(ysum_ready, b - SLOTS + 1)
                    load_results(b, n)
                    store_out(b - SLOTS)
            for n in range(SLOTS):
                store_out(B - SLOTS + n)
            sp.wait_ge(out_stored, 16 * B)

        @block.gpsimd
        def _(pool):
            nc.gpsimd.iota(offs[:], pattern=[[1, P]], base=0, channel_multiplier=-1).then_inc(pool_consts, 1)
            nc.gpsimd.iota(iota_ei[:], pattern=[[1, E]], base=0, channel_multiplier=0).then_inc(pool_consts, 1)
            nc.gpsimd.iota(token_i[:], pattern=[[TOPK * P, NT]], base=0, channel_multiplier=TOPK).then_inc(pool_consts, 1)
            nc.gpsimd.iota(it_i[:], pattern=[[1, EXPERT_TILES]], base=0, channel_multiplier=0).then_inc(pool_consts, 1)
            nc.gpsimd.memset(decay[:], DECAY).then_inc(pool_consts, 1)
            nc.gpsimd.memset(ones[:], 1.0).then_inc(pool_consts, 1)
            pool.wait_ge(pool_consts, 6)

            def store_rows(b, q):
                pool.wait_ge(rows_ready, b + 1)
                pool.wait_ge(ids_ready, b + 1)
                pool.wait_ge(slot_ready, b + 1)
                pool.nop(nofuse=True)
                for j in range(J):
                    for k in range(TOPK):
                        nc.gpsimd.indirect_dma_start(
                            out=rows_d, out_offset=bass.IndirectOffsetOnAxis(ap=slot[q][:, j, k:k + 1], axis=0),
                            in_=rows[q][:, j, :], in_offset=None).then_inc(rows_stored[q], 16)

            with pool.Fori(0, B - 1, 2) as b:
                for q in range(2):
                    store_rows(b + q, q)

            def store_results(i, q, first):
                pool.wait_ge(targets_ready, i + 1)
                if not first:
                    pool.wait_ge(results_stored[q], (i - q) * 8)
                nc.gpsimd.tensor_copy(target[q][:], targets[:, bass.ds(i, 1)]).then_inc(target_ready, 1)
                pool.wait_ge(target_ready, i + 1)
                pool.wait_ge(y_ready, i + 1)
                pool.nop(nofuse=True)
                nc.gpsimd.indirect_dma_start(
                    out=results_d, out_offset=bass.IndirectOffsetOnAxis(ap=target[q][:], axis=0),
                    in_=y[q][:], in_offset=None, bounds_check=TOPK * T - 1, oob_is_err=False,
                ).then_inc(results_stored[q], 16)

            for q in range(2):
                store_results(q, q, True)
            with pool.Fori(2, EXPERT_TILES - 1, 2) as i:
                for q in range(2):
                    store_results(i + q, q, False)

            with pool.Fori(0, B // 2) as pair:
                for q in range(2):
                    b = pair * 2 + q
                    pool.wait_ge(ygb_ready, b + 1)
                    nc.gpsimd.tensor_tensor(X[:, tiles(b), :], ygb[q][:], X[:, tiles(b), :], ALU.add).then_inc(o_ready, 1)

        @block.scalar
        def _(act):
            act.wait_ge(mod_loaded, 32)
            nc.scalar.activation(c_act[:], c_sb[:], ACT.Silu).then_inc(act_setup, 1)
            act.wait_ge(gains_loaded, 48)
            act.wait_ge(dve_setup, SETUP_PADDING)
            nc.scalar.activation(b1hi[:], b1f[:], ACT.Copy).then_inc(act_setup, 1)
            nc.scalar.activation(onesr[:], onesf[:], ACT.Copy).then_inc(act_setup, 1)

            act.wait_ge(dve_setup, SETUP_END)

            def normalise(b, dst, x_tiles, rs_, nm_, ready):
                for j in range(J):
                    ins = nc.scalar.activation(dst[:, j:j + 1, :], X[:, bass.ds(b * J + j, 1), :], ACT.Identity,
                                               bias=nm_[:, x_tiles + j:x_tiles + j + 1],
                                               scale=rs_[:, x_tiles + j:x_tiles + j + 1])
                ins.then_inc(ready, 1)

            def mixer_step(s, q, e):
                if on(s, B):
                    act.wait_ge(t1_done, s + 1)
                    nc.scalar.activation(h1T[q][:], bank[0][:], ACT.Identity, bias=mod[:, 0, bass.ds(s, 1)],
                                         scale=mod[:, 1, bass.ds(s, 1)]).then_inc(h1T_ready, 1)
                    if on(s - 2, B):
                        act.wait_ge(bias_done if q == 0 else means_done, e)
                    column = (be1T if q == 0 else g1m)[:, bass.ds(e * CF, CF)]
                    nc.scalar.activation(spread[q][:], column.rearrange("p (c o) -> p c o", o=1).broadcast_to([P, CF, P]),
                                         ACT.Copy).then_inc(spread_ready, 1)
                if on(s - 2, B):
                    act.wait_ge(nm_ready, s + 2)
                    normalise(s - 2, n2[q], 0, rs[1 - q], nm[1 - q], n2_ready)
                if on(s, B):
                    act.wait_ge(xi0_done, s + 1)
                    nc.scalar.activation(xi[q][:, 0, :], bank[1][:], ACT.Silu, bias=bcol[:, 0:1]).then_inc(xi0_ready, 1)
                    act.wait_ge(xi1_done, s + 1)
                    nc.scalar.activation(xi[q][:, 1, :], bank[2][:], ACT.Silu, bias=bcol[:, 1:2]).then_inc(xi1_ready, 1)
                if on(s - 2, B):
                    act.wait_ge(t2_done, s - 1)
                    nc.scalar.activation(h2T[q][:], bank[6][:], ACT.Identity, bias=mod[:, 3, bass.ds(s - 2, 1)],
                                         scale=mod[:, 4, bass.ds(s - 2, 1)]).then_inc(h2T_ready, 1)
                if on(s + 1, B):
                    act.wait_ge(nm_ready, s + 2)
                    normalise(s + 1, n1[1 - q], J, rs[1 - q], nm[1 - q], n1_ready)
                if on(s, B):
                    act.wait_ge(u_done, s + 1)
                    nc.scalar.activation(skip[q][:], bank[4][:], ACT.Identity, bias=ga_bout[:, bass.ds(s, 1)],
                                         scale=mod[:, 2, bass.ds(s, 1)]).then_inc(skip_ready, 1)
                if on(s - 2, B):
                    act.wait_ge(back_done, s - 1)
                    if on(s - 4, B):
                        act.wait_ge(rows_stored[q], (s - 2 - q) * (PER // 2))
                    nc.scalar.activation(rows[q][:, :, 0:D], bank[6][:].rearrange("p (j d) -> p j d", j=J),
                                         ACT.Copy).then_inc(rows_ready, 1)

            run(act, mixer_step, FIRST1, LOOP1, LAST1)

            def expert_step(s, q, _):
                if on(s + 1, EXPERT_TILES):
                    act.wait_ge(t3_done, s + 2)
                    nc.scalar.activation(h3T[1 - q][:], bank[0][:, 0:P], ACT.Copy).then_inc(h3T_ready, 1)
                if on(s, EXPERT_TILES):
                    act.wait_ge(h_done, s + 1)
                    nc.scalar.activation(r[q][:], bank[1 + q][:], ACT.Relu).then_inc(r_ready, 1)
                if on(s - 3, EXPERT_TILES):
                    act.wait_ge(v0_ready, s - 2)
                    if on(s - 5, EXPERT_TILES):
                        act.wait_ge(vg_ready, s - 4)
                    nc.scalar.activation(v[1 - q][:], v0[1 - q][:], ACT.Relu).then_inc(v_ready, 1)
                if on(s - 1, EXPERT_TILES):
                    act.wait_ge(tr_done, s)
                    nc.scalar.activation(rT[1 - q][:], bank[3][:], ACT.Copy).then_inc(rT_ready, 1)
                if on(s - 1, EXPERT_TILES) or on(s - 4, EXPERT_TILES):
                    n = norms(s)
                    act.wait_ge(mve_ready, s)
                    nc.scalar.activation(sde[q][:, n], mve[q][:, n, 1], ACT.Sqrt, bias=eps[:]).then_inc(sde_ready, 1)

            run(act, expert_step, FIRST2, LOOP2, LAST2)

            nc.scalar.activation(gate[:, 0, :], lead[:], ACT.Sigmoid)
            nc.scalar.activation(gate[:, 1, :], lead[:], ACT.Sigmoid, scale=-1.0).then_inc(gate_ready, 1)
            act.wait_ge(gate_ready, 1)

            def gate_first(b, n, loaded, first):
                q = n % 2
                act.wait_ge(y01_loaded[n], loaded)
                if not first:
                    act.wait_ge(ysum_ready, b - 1)
                for j in range(J):
                    ins = nc.scalar.activation(y0g[q][:, j, :], y01[n][:, j, 0:D], ACT.Copy,
                                               scale=gate[:, 0, bass.ds(b * J + j, 1)])
                ins.then_inc(y0g_ready, 1)

            for n in range(SLOTS):
                gate_first(n, n, 16, n < 2)
            with act.Fori(1, B // SLOTS) as turn:
                for n in range(SLOTS):
                    gate_first(turn * SLOTS + n, n, turn * 16 + 16, False)

        @block.vector
        def _(dve):
            vec = nc.vector
            done = [0]

            def mark(ins):
                ins.then_inc(dve_setup, 1)
                done[0] += 1

            dve.wait_ge(pool_consts, 6)
            vec.tensor_scalar(ident[:], offs[:], 0.0, None, ALU.is_equal)
            vec.tensor_scalar(before[:], offs[:], 0.0, None, ALU.is_gt)
            vec.tensor_copy(iota_e[:], iota_ei[:])
            vec.tensor_scalar(base_e[:], iota_ei[:], float(REGION), None, ALU.mult)
            vec.tensor_copy(token[:], token_i[:])
            vec.tensor_copy(it_f[:], it_i[:])
            vec.memset(carry[:], 0.0)
            vec.memset(onesf[:], 1.0)
            vec.memset(ones_e[:], 1.0)
            vec.memset(eps[:], EPS)
            mark(vec.memset(padding[:], 0.0))
            dve.wait_ge(dve_setup, 1)
            mark(vec.memset(padding[:, D:D + 1], NOWHERE))
            assert done[0] == SETUP_PADDING
            dve.wait_ge(pe_setup, 1)
            mark(vec.tensor_copy(cT[:], bank[0][:, 0:B]))
            assert done[0] == SETUP_CT
            dve.wait_ge(pe_setup, 2)
            m = bank[1][:, 0:5 * B].rearrange("p (m b) -> p m b", m=5)
            vec.tensor_copy(mod[:, 0, :], m[:, 0, :])
            vec.tensor_scalar(mod[:, 1, :], m[:, 1, :], 1.0, None, ALU.add)
            vec.tensor_copy(mod[:, 3, :], m[:, 3, :])
            vec.tensor_scalar(mod[:, 4, :], m[:, 4, :], 1.0, None, ALU.add)
            vec.tensor_scalar(mod_sign[:], m[:, 2, :], 0.0, 2.0, ALU.is_ge, ALU.mult)
            mark(vec.tensor_scalar(gb_sign[:], bank[2][0:B, 0:D], 0.0, 2.0, ALU.is_ge, ALU.mult))
            dve.wait_ge(dve_setup, 4)
            vec.tensor_scalar(mod_sign[:], mod_sign[:], -1.0, None, ALU.add)
            mark(vec.tensor_scalar(gb_sign[:], gb_sign[:], -1.0, None, ALU.add))
            dve.wait_ge(dve_setup, 5)
            vec.tensor_tensor(mod_abs[:], mod_sign[:], m[:, 2, :], ALU.mult)
            mark(vec.tensor_tensor(gb_abs[:], gb_sign[:], bank[2][0:B, 0:D], ALU.mult))
            dve.wait_ge(dve_setup, 6)
            vec.scalar_tensor_tensor(mod[:, 2, :], mod_abs[:], 0.25, mod_sign[:], ALU.max, ALU.mult)
            mark(vec.scalar_tensor_tensor(gb_raw[:], gb_abs[:], 0.25, gb_sign[:], ALU.max, ALU.mult))
            assert done[0] == SETUP_GB
            dve.wait_ge(dve_setup, 7)
            dve.wait_ge(small_loaded, 16 * 9)
            vec.tensor_scalar(ga_bout[:], mod[:, 2, :], boutc[:], None, ALU.mult)
            dve.wait_ge(pe_setup, 3)
            mark(vec.tensor_tensor(cpT[:], bank[3][:, 0:CI * NS].rearrange("p (c s) -> p c s", c=CI), bp[:], ALU.mult))
            dve.wait_ge(dve_setup, 8)
            mark(vec.tensor_reduce(ccol[:], cpT[:], axis=AX, op=ALU.add))
            dve.wait_ge(dve_setup, 9)
            for ch in range(CI):
                vec.tensor_scalar(wz[:, ch, :], wout[:, ch, :], ccol[:, ch:ch + 1], None, ALU.mult)
                ins = vec.tensor_scalar(wu[:, ch, :], wout[:, ch, :], dcol[:, ch:ch + 1], None, ALU.mult)
            mark(ins)
            dve.wait_ge(pe_setup, 4)
            vec.tensor_copy(g1T[:], bank[4][:, 0:E * CF])
            vec.tensor_scalar(g1m[:], bank[4][:, 0:E * CF], 1.0 / F, None, ALU.mult)
            mark(vec.tensor_copy(be1T[:], bank[4][:, E * CF:2 * E * CF]))
            dve.wait_ge(act_setup, 2)
            mark(vec.tensor_tensor(b1lo[:], b1f[:], b1hi[:], ALU.subtract))
            assert done[0] == SETUP_END

            def mixer_step(s, q, e):
                p = 1 - q
                both = slice(0 if on(s - 1, B) else J, 2 * J if on(s + 2, B) else J)
                a, b, c = s - 1, s + 2, s - 3
                any_norm = on(a, B) or on(b, B)
                if on(a, B):
                    dve.wait_ge(z_done, s)
                    vec.tensor_tensor_scan(scan[p][:], decay[:], bank[3][:], 0.0, ALU.mult, ALU.add).then_inc(scan_ready, 1)
                if on(c, B):
                    dve.wait_ge(logit_done, c + 1)
                    vec.tensor_tensor(logit[p][:], bank[7][:, 0:J * E].rearrange("p (j e) -> p j e", j=J),
                                      br[:].rearrange("p (o e) -> p o e", o=1).broadcast_to([P, J, E]),
                                      ALU.add).then_inc(logit_ready, 1)
                if on(a, B):
                    dve.wait_ge(skip_ready, s)
                    dve.wait_ge(scan_ready, s)
                    vec.scalar_tensor_tensor(mixT[p][:], scan[p][:], mod[:, 2, bass.ds(a, 1)], skip[p][:],
                                             ALU.mult, ALU.add).then_inc(mix_ready, 1)
                if on(c, B):
                    dve.wait_ge(logit_ready, c + 1)
                    dve.nop(nofuse=True)
                    for j in range(J):
                        ins = vec.max(best[p][:, j, :], logit[p][:, j, :])
                    ins.then_inc(best_ready, 1)
                if on(b, B):
                    if isinstance(b, int):
                        for n in range(XL):
                            if b * J * XL // NT == n or (b == LOOP1[0] + 1 and n > 0):
                                dve.wait_ge(x_loaded[n], 16)
                    for j in range(J):
                        ins = vec.bn_stats(st[q][:, J + j, :], X[:, bass.ds(b * J + j, 1), :])
                    if not on(a, B):
                        ins.then_inc(stats_ready, 1)
                if on(c, B):
                    dve.wait_ge(best_ready, c + 1)
                    dve.nop(nofuse=True)
                    for j in range(J):
                        ins = vec.max_index(besti[p][:, j, :], best[p][:, j, :], logit[p][:, j, :])
                    ins.then_inc(besti_ready, 1)
                if on(a, B):
                    xa = X[:, tiles(a), :]
                    dve.wait_ge(mix_done, s)
                    vec.tensor_tensor(xa, xa, bank[5][:].rearrange("p (j d) -> p j d", j=J), ALU.add).then_inc(x1_ready, 1)
                if on(c, B):
                    dve.wait_ge(besti_ready, c + 1)
                    vec.tensor_tensor(
                        hot[p][:], iota_e[:].rearrange("p (a b e) -> p a b e", a=1, b=1).broadcast_to([P, J, TOPK, E]),
                        besti[p][:, :, 0:TOPK].rearrange("p j (k o) -> p j k o", o=1).broadcast_to([P, J, TOPK, E]),
                        ALU.is_equal).then_inc(hot_ready, 1)
                    vec.tensor_tensor(lead[:, tiles(c)], best[p][:, :, 0], best[p][:, :, 1], ALU.subtract)
                    if on(c - 2, B):
                        dve.wait_ge(rows_stored[p], (c - p) * (PER // 2))
                    vec.tensor_copy(rows[p][:, :, D], token[:, tiles(c)])
                    dve.wait_ge(hot_ready, c + 1)
                    vec.tensor_tensor(hots[p][:], hot[p][:, :, 0, :], hot[p][:, :, 1, :], ALU.add).then_inc(hots_ready, 1)
                    vec.tensor_copy(rows[p][:, :, D + 1], besti[p][:, :, 0]).then_inc(ids_ready, 1)
                if on(a, B):
                    dve.wait_ge(x1_ready, s)
                    dve.nop(nofuse=True)
                    for j in range(J):
                        ins = vec.bn_stats(st[q][:, j, :], X[:, bass.ds(a * J + j, 1), :])
                    ins.then_inc(stats_ready, 1)
                def square(n):
                    if any_norm:
                        dve.wait_ge(newton[n - 1][2] if n else guess_ready, s + 3)
                        vec.tensor_tensor(sq[q][:, both], rs[q][:, both], rs[q][:, both], ALU.mult).then_inc(newton[n][0], 1)

                def times_v(n):
                    if any_norm:
                        dve.wait_ge(newton[n][0], s + 3)
                        vec.scalar_tensor_tensor(hv[q][:, both], sq[q][:, both], -0.5, ve[q][:, both], ALU.mult,
                                                 ALU.mult).then_inc(newton[n][1], 1)

                def refine(n):
                    if any_norm:
                        dve.wait_ge(newton[n][1], s + 3)
                        vec.scalar_tensor_tensor(rs[q][:, both], hv[q][:, both], 1.5, rs[q][:, both], ALU.add,
                                                 ALU.mult).then_inc(newton[n][2], 1)

                def weights(ch):
                    if on(s, B) and q == 0 and ch == 0:
                        if isinstance(s, int) and s == 0:
                            dve.wait_ge(b2_loaded, 16)
                        dve.wait_ge(bias_done, e + 1)
                        vec.tensor_tensor(c2[:, bass.ds(e, 1), :], bank[0][:, 0:D].rearrange("p (o d) -> p o d", o=1),
                                          c2[:, bass.ds(e, 1), :], ALU.add).then_inc(c2_ready, 1)
                    if on(s, B) and q == 1:
                        if ch == 0:
                            dve.wait_ge(means_done, e + 1)
                        w = W2[:, bass.ds(e * CF + ch, 1), :]
                        ins = vec.scalar_tensor_tensor(
                            w, w, g1T[:, bass.ds(e * CF + ch, 1)], bank[0][:, 0:D].rearrange("p (o d) -> p o d", o=1),
                            ALU.mult, ALU.subtract)
                        if ch == CF - 1:
                            ins.then_inc(w2_ready, 1)

                if any_norm:
                    dve.wait_ge(stats_ready, s + 3)
                    dve.nop(nofuse=True)
                    for j in range(both.start, both.stop):
                        ins = vec.bn_aggr(mv[q][:, j, :], st[q][:, j, :])
                    ins.then_inc(mv_ready, 1)
                if on(c, B):
                    dve.wait_ge(hots_ready, c + 1)
                    vec.tensor_reduce(hotsum[p][:], hots[p][:].rearrange("p j e -> p e j"), axis=AX,
                                      op=ALU.add).then_inc(hotsum_ready, 1)
                if any_norm:
                    dve.wait_ge(mv_ready, s + 3)
                    vec.tensor_scalar(ve[q][:, both], mv[q][:, both, 1], EPS, None, ALU.add).then_inc(ve_ready, 1)
                weights(0)
                if any_norm:
                    dve.wait_ge(ve_ready, s + 3)
                    vec.tensor_scalar(rs[q][:, both].bitcast(I32), ve[q][:, both].bitcast(I32), -0.5, float(0x5F3759DF),
                                      ALU.mult, ALU.add).then_inc(guess_ready, 1)
                weights(1)
                square(0)
                weights(2)
                times_v(0)
                weights(3)
                refine(0)
                if on(c, B):
                    dve.wait_ge(rank_done, c + 1)
                    vec.tensor_tensor(place[p][:], bank[7][:, J * E:2 * J * E].rearrange("p (j e) -> p j e", j=J),
                                      base_e[:].rearrange("p (o e) -> p o e", o=1).broadcast_to([P, J, E]),
                                      ALU.add).then_inc(place_ready, 1)
                square(1)
                if on(c, B):
                    dve.wait_ge(hotsum_ready, c + 1)
                    vec.tensor_tensor(carry[:], carry[:], hotsum[p][:], ALU.add).then_inc(carry_ready, 1)
                times_v(1)
                if on(c, B):
                    dve.wait_ge(place_ready, c + 1)
                    vec.tensor_tensor(placed[p][:], hot[p][:],
                                      place[p][:].rearrange("p j (o e) -> p j o e", o=1).broadcast_to([P, J, TOPK, E]),
                                      ALU.mult).then_inc(placed_ready, 1)
                refine(1)
                square(2)
                if on(c, B):
                    dve.wait_ge(placed_ready, c + 1)
                    with nc.allow_low_precision(reason="one whole number below 2**24 and zeros"):
                        vec.tensor_reduce(slot[p][:], placed[p][:], axis=AX, op=ALU.add).then_inc(slot_ready, 1)
                times_v(2)
                refine(2)
                if any_norm:
                    dve.wait_ge(newton[2][2], s + 3)
                    vec.scalar_tensor_tensor(nm[q][:, both], mv[q][:, both, 0], -1.0, rs[q][:, both], ALU.mult,
                                             ALU.mult).then_inc(nm_ready, 1)

            run(dve, mixer_step, FIRST1, LOOP1, LAST1)

            ticks = [0]

            def link(ins):
                ins.then_inc(table_step, 1)
                ticks[0] += 1
                dve.wait_ge(table_step, ticks[0])

            dve.wait_ge(count_done, 1)
            vec.tensor_copy(cnt_i[:], bank[7][:, 0:E])
            link(vec.tensor_scalar(cnt[:], bank[7][:, 0:E], float(P - 1), None, ALU.add))
            link(vec.tensor_copy(nt_i[:], cnt[:]))
            link(vec.tensor_scalar(nt_i[:], nt_i[:], P.bit_length() - 1, None, ALU.logical_shift_right))
            link(vec.tensor_copy(nt_f[:], nt_i[:]))
            vec.tensor_scalar(jump[:], nt_f[:], -float(P), float(REGION), ALU.mult, ALU.add)
            link(vec.tensor_tensor_scan(ends[:], ones_e[:], nt_f[:], 0.0, ALU.mult, ALU.add))
            for e in range(E):
                vec.tensor_scalar(past[:, e, :], it_f[:], ends[:, e:e + 1], None, ALU.is_ge)
                ins = vec.tensor_scalar(hop[:, e, :], it_f[:], ends[:, e:e + 1], jump[:, e:e + 1], ALU.is_ge, ALU.mult)
            link(ins)
            vec.tensor_reduce(tile_e[:], past[:].rearrange("p e i -> p i e"), axis=AX, op=ALU.add)
            link(vec.tensor_reduce(tile_hop[:], hop[:].rearrange("p e i -> p i e"), axis=AX, op=ALU.add))
            vec.tensor_scalar(tile_ei[:], tile_e[:], float(E - 1), None, ALU.min)
            vec.scalar_tensor_tensor(tile_row[:], it_f[:], float(P), tile_hop[:], ALU.mult, ALU.add).then_inc(table_ready, 1)
            dve.wait_ge(table_ready, 1)

            dve.wait_ge(rows_loaded, 32)

            def wide(ap):
                return ap.rearrange("p (o d) -> p o d", o=1)

            def target_of(i, q):
                dve.wait_ge(hrow_loaded[q], (i + 2 - q) * 8)
                vec.scalar_tensor_tensor(targets[:, bass.ds(i, 1)], hrow[q][:, D + 1:D + 2], tile_e[:, bass.ds(i, 1)],
                                         hrow[q][:, D:D + 1], ALU.not_equal, ALU.add).then_inc(targets_ready, 1)

            def expert_step(s, q, expert):
                p = 1 - q
                if on(s - 2, EXPERT_TILES) or on(s - 5, EXPERT_TILES):
                    n = norms(s - 1)
                    dve.wait_ge(sde_ready, s - 1)
                    vec.reciprocal(rse[p][:, n], sde[p][:, n]).then_inc(rse_ready, 1)
                if on(s - 5, EXPERT_TILES):
                    e = expert(-5)
                    vec.scalar_tensor_tensor(wide(vg[p][:]), wide(v[p][:]), mve[p][:, 1, 0:1], g2[:, bass.ds(e, 1), :],
                                             ALU.subtract, ALU.mult).then_inc(vg_ready, 1)
                if on(s - 3, EXPERT_TILES):
                    e3 = expert(-3)
                    dve.wait_ge(y_done, s - 2)
                    dve.wait_ge(rse_ready, s - 2)
                    vec.scalar_tensor_tensor(wide(v0[p][:]), wide(bank[4 + p][:, 0:D]), rse[q][:, 0:1],
                                             c2[:, bass.ds(e3, 1), :], ALU.mult, ALU.add).then_inc(v0_ready, 1)
                if on(s - 1, EXPERT_TILES):
                    dve.wait_ge(r_ready, s)
                    dve.nop(nofuse=True)
                    vec.bn_stats(stf[p][:], r[p][:]).then_inc(stf_ready, 1)
                if on(s - 4, EXPERT_TILES):
                    dve.wait_ge(v_ready, s - 3)
                    dve.nop(nofuse=True)
                    vec.bn_stats(sty[q][:], v[q][:]).then_inc(sty_ready, 1)
                if on(s - 5, EXPERT_TILES):
                    dve.wait_ge(vg_ready, s - 4)
                    dve.wait_ge(rse_ready, s - 1)
                    if on(s - 7, EXPERT_TILES):
                        dve.wait_ge(results_stored[p], (s - 5 - p) * 8)
                    vec.scalar_tensor_tensor(wide(y[p][:]), wide(vg[p][:]), rse[p][:, 1:2], be2[:, bass.ds(e, 1), :],
                                             ALU.mult, ALU.add).then_inc(y_ready, 1)
                if on(s + 1, EXPERT_TILES):
                    target_of(s + 1, p)
                if on(s - 1, EXPERT_TILES):
                    dve.wait_ge(stf_ready, s)
                    dve.nop(nofuse=True)
                    ins = vec.bn_aggr(mve[q][:, 0, :], stf[p][:])
                if on(s - 4, EXPERT_TILES):
                    dve.wait_ge(sty_ready, s - 3)
                    dve.nop(nofuse=True)
                    ins = vec.bn_aggr(mve[q][:, 1, :], sty[q][:])
                if on(s - 1, EXPERT_TILES) or on(s - 4, EXPERT_TILES):
                    ins.then_inc(mve_ready, 1)

            run_tiles(mybir.EngineType.DVE, dve, expert_step, -5)

            dve.wait_ge(gate_ready, 1)
            dve.wait_ge(gb_loaded, 16)

            def sums(b, n, first):
                q = n % 2
                dve.wait_ge(y0g_ready, b + 1)
                for j in range(J):
                    ins = vec.scalar_tensor_tensor(ysum[q][:, j, :], y01[n][:, j, D:2 * D], gate[:, 1, bass.ds(b * J + j, 1)],
                                                   y0g[q][:, j, :], ALU.mult, ALU.add)
                ins.then_inc(ysum_ready, 1)
                dve.wait_ge(ysum_ready, b + 1)
                if not first:
                    dve.wait_ge(o_ready, b - 1)
                vec.tensor_tensor(ygb[q][:], ysum[q][:], gb_rows[:, bass.ds(b, 1), :].broadcast_to([P, J, D]),
                                  ALU.mult).then_inc(ygb_ready, 1)

            for n in range(SLOTS):
                sums(n, n, n < 2)
            with dve.Fori(1, B // SLOTS) as turn:
                for n in range(SLOTS):
                    sums(turn * SLOTS + n, n, False)

        @block.tensor
        def _(pe):
            mm, tr = nc.tensor.matmul, nc.tensor.transpose
            pe.wait_ge(dve_setup, SETUP_PADDING)
            pe.wait_ge(act_setup, 1)
            tr(bank[0][:, 0:B], c_act[:], ident[0:B, 0:B]).then_inc(pe_setup, 1)
            pe.wait_ge(dve_setup, SETUP_CT)
            for n in range(5):
                mm(bank[1][:, n * B:(n + 1) * B], wmod[:, n * D:(n + 1) * D], cT[:], start=True, stop=True)
            mm(bank[2][0:B, 0:D], cT[:], wmod[:, 5 * D:6 * D], start=True, stop=True).then_inc(pe_setup, 1)
            pe.wait_ge(small_loaded, 16 * 9)
            for ch in range(CI):
                ins = tr(bank[3][:, ch * NS:(ch + 1) * NS], cp[:, ch * P:(ch + 1) * P], ident[0:NS, 0:NS])
            ins.then_inc(pe_setup, 1)
            pe.wait_ge(gains_loaded, 48)
            tr(bank[4][:, 0:E * CF], g1r[:], ident[0:E * CF, 0:E * CF])
            tr(bank[4][:, E * CF:2 * E * CF], be1r[:], ident[0:E * CF, 0:E * CF]).then_inc(pe_setup, 1)
            pe.wait_ge(dve_setup, SETUP_END)

            def transpose_batch(to, of):
                for j in range(J):
                    ins = tr(bank[to][:, j * P:(j + 1) * P], of(j), ident[:])
                return ins

            def mixer_step(s, q, e):
                p = 1 - q
                if on(s, B):
                    pe.wait_ge(n1_ready, s + 1)
                    if q == 0 and on(s - 1, B):
                        pe.wait_ge(w2_ready, e)
                    if q == 1:
                        pe.wait_ge(c2_ready, e + 1)
                    transpose_batch(0, lambda j: n1[q][:, j, :]).then_inc(t1_done, 1)
                if on(s - 1, B):
                    pe.wait_ge(mix_ready, s)
                    transpose_batch(5, lambda j: mixT[p][:, j * P:(j + 1) * P]).then_inc(mix_done, 1)
                if on(s, B):
                    pe.wait_ge(h1T_ready, s + 1)
                    mm(bank[1][:], win[:, 0:P], h1T[q][:], start=True, stop=True).then_inc(xi0_done, 1)
                    mm(bank[2][:], win[:, P:2 * P], h1T[q][:], start=True, stop=True).then_inc(xi1_done, 1)
                    if isinstance(s, int) and s == 0:
                        pe.wait_ge(w2_loaded, 16)
                    pe.wait_ge(spread_ready, s + 1)
                    for ch in range(CF):
                        ins = mm(bank[0][:, 0:D].rearrange("p (o d) -> p o d", o=1),
                                 spread[q][:, ch, :], W2[:, bass.ds(e * CF + ch, 1), :],
                                 start=(ch == 0), stop=(ch == CF - 1))
                    ins.then_inc(bias_done if q == 0 else means_done, 1)
                if on(s - 2, B):
                    pe.wait_ge(n2_ready, s - 1)
                    if on(s - 3, B):
                        pe.wait_ge(rows_ready, s - 2)
                    transpose_batch(6, lambda j: n2[q][:, j, :]).then_inc(t2_done, 1)
                if on(s - 3, B):
                    acc = bank[7][:, J * E:2 * J * E].rearrange("p (j e) -> p j e", j=J)
                    pe.wait_ge(hots_ready, s - 2)
                    mm(acc, before[:], hots[p][:], start=True, stop=False)
                    for j in range(J - 1):
                        mm(acc[:, j + 1:J, :], ones[:], hots[p][:, j:j + 1, :].broadcast_to([P, J - 1 - j, E]),
                           start=False, stop=False)
                    if on(s - 4, B):
                        pe.wait_ge(carry_ready, s - 3)
                    mm(acc, ones[:], carry[:].rearrange("p (o e) -> p o e", o=1).broadcast_to([P, J, E]),
                       start=False, stop=True).then_inc(rank_done, 1)
                if on(s, B):
                    pe.wait_ge(xi0_ready, s + 1)
                    mm(bank[3][:], wz[:, 0, :], xi[q][:, 0, :], start=True, stop=False)
                    pe.wait_ge(xi1_ready, s + 1)
                    mm(bank[3][:], wz[:, 1, :], xi[q][:, 1, :], start=False, stop=True).then_inc(z_done, 1)
                    mm(bank[4][:], wu[:, 0, :], xi[q][:, 0, :], start=True, stop=False)
                    mm(bank[4][:], wu[:, 1, :], xi[q][:, 1, :], start=False, stop=True).then_inc(u_done, 1)
                if on(s - 2, B):
                    pe.wait_ge(h2T_ready, s - 1)
                    if on(s - 3, B):
                        pe.wait_ge(place_ready, s - 2)
                    for j in range(J):
                        ins = mm(bank[7][:, j * E:(j + 1) * E], h2T[q][:, j * P:(j + 1) * P], wr[:], start=True, stop=True)
                    ins.then_inc(logit_done, 1)
                    transpose_batch(6, lambda j: h2T[q][:, j * P:(j + 1) * P]).then_inc(back_done, 1)

            run(pe, mixer_step, FIRST1, LOOP1, LAST1)
            pe.wait_ge(carry_ready, B)
            pe.wait_ge(place_ready, B)
            mm(bank[7][:, 0:E], ones[:], carry[:], start=True, stop=True).then_inc(count_done, 1)

            pe.wait_ge(w1_loaded, 16)
            pe.wait_ge(b1_stored, 32)
            pe.wait_ge(table_ready, 1)

            def expert_step(s, q, expert):
                p = 1 - q
                if on(s + 1, EXPERT_TILES):
                    pe.wait_ge(hrow_loaded[p], (s + 3 - p) * 8)
                    if on(s, EXPERT_TILES):
                        pe.wait_ge(h3T_ready, s + 1)
                    tr(bank[0][:, 0:P], hrow[p][:, 0:D], ident[:]).then_inc(t3_done, 1)
                if on(s, EXPERT_TILES):
                    e = expert(0)
                    h = bank[1 + q][:].rearrange("p (o f) -> p o f", o=1)
                    pe.wait_ge(h3T_ready, s + 1)
                    if on(s - 2, EXPERT_TILES):
                        pe.wait_ge(r_ready, s - 1)
                    mm(h, onesr[:], b1_parts[:, bass.ds(e, 1), :], start=True, stop=False)
                    mm(h, h3T[q][:], W1[:, bass.ds(e, 1), :], start=False, stop=True).then_inc(h_done, 1)
                if on(s - 1, EXPERT_TILES):
                    pe.wait_ge(r_ready, s)
                    if on(s - 2, EXPERT_TILES):
                        pe.wait_ge(rT_ready, s - 1)
                    for ch in range(CF):
                        ins = tr(bank[3][:, ch * P:(ch + 1) * P], r[p][:, ch * P:(ch + 1) * P], ident[:])
                    ins.then_inc(tr_done, 1)
                if on(s - 2, EXPERT_TILES):
                    e2 = expert(-2)
                    acc = bank[4 + q][:, 0:D].rearrange("p (o d) -> p o d", o=1)
                    pe.wait_ge(rT_ready, s - 1)
                    if on(s - 4, EXPERT_TILES):
                        pe.wait_ge(v0_ready, s - 3)
                    for ch in range(CF):
                        ins = mm(acc, rT[q][:, ch * P:(ch + 1) * P], W2[:, bass.ds(e2 * CF + ch, 1), :],
                                 start=(ch == 0), stop=(ch == CF - 1))
                    ins.then_inc(y_done, 1)

            run_tiles(mybir.EngineType.PE, pe, expert_step, -2)


SETUP_PADDING, SETUP_CT, SETUP_GB, SETUP_END = 2, 3, 7, 12

_INS = ['L0_attn_x', 'L0_attn_Win', 'L0_attn_bin_', 'L0_attn_Bp', 'L0_attn_Cp', 'L0_attn_Dp', 'L0_attn_Wout',
        'L0_attn_bout', 'L0_ffn_Wr', 'L0_ffn_br', 'L0_ffn_W1', 'L0_ffn_b1', 'L0_ffn_g1', 'L0_ffn_be1', 'L0_ffn_W2',
        'L0_ffn_b2', 'L0_ffn_g2', 'L0_ffn_be2', 'L0_c', 'L0_wmod']


def kernel(**inputs):
    import numpy as _np
    import concourse.bacc as _bacc
    from concourse.bass_utils import run_bass_kernel_spmd as _run

    nc = _bacc.Bacc("TRN2", target_bir_lowering=False, num_devices=1)
    arrays, args = {}, []
    for name in _INS:
        a = _np.ascontiguousarray(inputs[name])
        arrays[f"in_{name}"] = a
        args.append(nc.dram_tensor(f"in_{name}", a.shape, mybir.dt.from_np(a.dtype), kind="ExternalInput").ap())
    shape = tuple(inputs['L0_attn_x'].shape)
    args.append(nc.dram_tensor("out_x", shape, mybir.dt.float32, kind="ExternalOutput").ap())
    adaln_ssm_moe_kernel(nc, *args)
    r = _run(nc, [arrays], core_ids=[0])
    return r.results[0]["out_x"]
```

```python
from contextlib import ExitStack

import concourse.bass as bass
from concourse import mybir


def adaln_ssm_moe_kernel(nc, x_in, win_in, bin_in, bp_in, cp_in, dp_in, wout_in, bout_in, wr_in, br_in,
                         w1_in, b1_in, g1_in, be1_in, w2_in, b2_in, g2_in, be2_in, c_in, wmod_in, out):
    F32, F32R, BF16 = mybir.dt.float32, mybir.dt.float32r, mybir.dt.bfloat16
    I32, U32 = mybir.dt.int32, mybir.dt.uint32
    ALU = mybir.AluOpType
    ACT = mybir.ActivationFunctionType
    AX = mybir.AxisListType.X

    B, L, D = x_in.shape
    P = 128
    J = L // P
    T = B * L
    NT = T // P
    DI, NS = bp_in.shape
    CI = DI // P
    E, _, F = w1_in.shape
    CF = F // P
    TOPK = 2
    EPS = 1e-5
    DECAY = 0.9
    REGION = T + P
    EXPERT_TILES = TOPK * NT + E - 1
    SPARE = E * REGION
    NSPARE = EXPERT_TILES - TOPK * NT
    ROW = D + 2
    NOWHERE = 65536.0
    assert D == P and B % 8 == 0 and E * CF == 4 * J * TOPK

    x_v = x_in.rearrange("b l d -> (b l) d").rearrange("(n p) d -> p n d", p=P)
    out_v = out.rearrange("b l d -> (b l) d").rearrange("(n p) d -> p n d", p=P)
    rows_d = nc.dram_tensor("expert_rows", (SPARE + NSPARE * P, ROW), F32, kind="Internal").ap()
    results_d = nc.dram_tensor("expert_results", (TOPK * T, D), F32, kind="Internal").ap()
    results_v = results_d.rearrange("(n p k) d -> p n (k d)", p=P, k=TOPK)
    sums_d = nc.dram_tensor("column_sums", (2, E, D), F32, kind="Internal").ap()
    gates_d = nc.dram_tensor("gate_b_rows", (1, B * D), F32, kind="Internal").ap()

    with ExitStack() as ctx:
        def sb(name, shape, dt=F32):
            return ctx.enter_context(nc.sbuf_tensor(name, shape, dt))

        def sem(name):
            return ctx.enter_context(nc.semaphore(name))

        bank = [ctx.enter_context(nc.psum_tensor(f"bank{n}", [P, 512], F32)) for n in range(8)]

        X = sb("X", [P, NT, D])
        W1hi = sb("W1hi", [P, E, F], F32R)
        W1lo = sb("W1lo", [P, E, F], F32R)
        W2 = sb("W2", [P, E * CF, D])
        c2 = sb("c2", [P, E, D])
        g2 = sb("g2", [P, E, D])
        be2 = sb("be2", [P, E, D])
        gb_rows = sb("gb_rows", [P, B, D])
        win = sb("win", [P, DI])
        wout = sb("wout", [P, CI, D])
        wz = sb("wz", [P, CI, D])
        wu = sb("wu", [P, CI, D])
        wr = sb("wr", [P, E])
        br = sb("br", [P, E])
        wmod = sb("wmod", [P, 6 * D])
        bcol = sb("bcol", [P, CI])
        dcol = sb("dcol", [P, CI])
        boutc = sb("boutc", [P, 1])
        bp = sb("bp", [P, CI, NS])
        cp = sb("cp", [NS, DI])
        cpT = sb("cpT", [P, CI, NS])
        ccol = sb("ccol", [P, CI])
        c_sb = sb("c_sb", [B, D])
        c_act = sb("c_act", [B, D])
        cT = sb("cT", [P, B])
        mod = sb("mod", [P, 5, B])
        mod_sign = sb("mod_sign", [P, B])
        mod_abs = sb("mod_abs", [P, B])
        ga_bout = sb("ga_bout", [P, B])
        gb_raw = sb("gb_raw", [B, D])
        gb_sign = sb("gb_sign", [B, D])
        gb_abs = sb("gb_abs", [B, D])
        g1r = sb("g1r", [E * CF, P])
        be1r = sb("be1r", [E * CF, P])
        g1T = sb("g1T", [P, E * CF])
        be1_g1m = sb("be1_g1m", [P, E * CF, 2])
        means = gb_rows
        b2_rows = c2[0:2, :, :]
        w2_sums = means[0:2, 0:E, :]
        b1f = sb("b1f", [E, F])
        b1hi = sb("b1hi", [E, F], F32R)
        b1lo = sb("b1lo", [E, F], F32R)
        b1_parts = sb("b1_parts", [2, E, F], F32R)
        onesr = sb("onesr", [2, P], F32R)
        onesf = sb("onesf", [2, P])
        offs = sb("offs", [P, P], I32)
        ident = sb("ident", [P, P])
        before = sb("before", [P, P], BF16)
        ones = sb("ones", [P, P], BF16)
        decay = sb("decay", [P, L])
        eps = sb("eps", [P, 1])
        root_of_eps = sb("root_of_eps", [P, 1])
        iota_e = sb("iota_e", [P, E])
        iota_ei = sb("iota_ei", [P, E], I32)
        base_e = sb("base_e", [P, E])
        token_i = sb("token_i", [P, NT], I32)
        token = sb("token", [P, NT])
        padding = sb("padding", [P, ROW])
        lead = sb("lead", [P, NT])
        n1 = [sb(f"n1_{q}", [P, J, D]) for q in range(2)]
        h1T = [sb(f"h1T_{q}", [P, L]) for q in range(2)]
        xi = [sb(f"xi_{q}", [P, CI, L]) for q in range(2)]
        scan = [sb(f"scan_{q}", [P, L]) for q in range(2)]
        skip = [sb(f"skip_{q}", [P, L]) for q in range(2)]
        mixT = [sb(f"mixT_{q}", [P, L]) for q in range(2)]
        st = [sb(f"st_{q}", [P, 2 * J, 6]) for q in range(2)]
        mv = [sb(f"mv_{q}", [P, 2 * J, 2]) for q in range(2)]
        ve = [sb(f"ve_{q}", [P, 2 * J]) for q in range(2)]
        sq = [sb(f"sq_{q}", [P, 2 * J]) for q in range(2)]
        hv = [sb(f"hv_{q}", [P, 2 * J]) for q in range(2)]
        rs = [sb(f"rs_{q}", [P, 2 * J]) for q in range(2)]
        nm = [sb(f"nm_{q}", [P, 2 * J]) for q in range(2)]
        n2 = [sb(f"n2_{q}", [P, J, D]) for q in range(2)]
        h2T = [sb(f"h2T_{q}", [P, L]) for q in range(2)]
        rows = [sb(f"rows_{q}", [P, J, ROW]) for q in range(2)]
        logit = [sb(f"logit_{q}", [P, J, E]) for q in range(2)]
        best = [sb(f"best_{q}", [P, J, 8]) for q in range(2)]
        besti = [sb(f"besti_{q}", [P, J, 8], U32) for q in range(2)]
        hot = [sb(f"hot_{q}", [P, J, TOPK, E]) for q in range(2)]
        hots = [sb(f"hots_{q}", [P, J, E], BF16) for q in range(2)]
        hotsum = [sb(f"hotsum_{q}", [P, E]) for q in range(2)]
        carry = sb("carry", [P, E], BF16)
        place = [sb(f"place_{q}", [P, J, E]) for q in range(2)]
        placed = [sb(f"placed_{q}", [P, J, TOPK, E]) for q in range(2)]
        slot = [sb(f"slot_{q}", [P, J, TOPK], I32) for q in range(2)]
        cnt = sb("cnt", [P, E])
        cnt_i = sb("cnt_i", [P, E], I32)
        nt_i = sb("nt_i", [P, E], I32)
        nt_f = sb("nt_f", [P, E])
        ends = sb("ends", [P, E])
        ones_e = sb("ones_e", [P, E])
        jump = sb("jump", [P, E])
        it_i = sb("it_i", [P, EXPERT_TILES], I32)
        it_f = sb("it_f", [P, EXPERT_TILES])
        past = sb("past", [P, E, EXPERT_TILES])
        hop = sb("hop", [P, E, EXPERT_TILES])
        W1E = 2
        w1_raw = [t[:].rearrange("p e i -> p (e i)")[:, 0:W1E * F].rearrange("p (e f) -> p e f", e=W1E)
                  for t in (past, hop)]
        tile_e = sb("tile_e", [P, EXPERT_TILES])
        tile_hop = sb("tile_hop", [P, EXPERT_TILES])
        pe_experts = sb("pe_experts", [P, 4 + EXPERT_TILES], I32)
        dve_experts = sb("dve_experts", [P, 4 + EXPERT_TILES], I32)
        pool_experts = sb("pool_experts", [P, EXPERT_TILES], I32)
        tile_row = sb("tile_row", [P, EXPERT_TILES], I32)
        SLOTS = 4
        hrow = [rows[0][:, n, :] for n in range(SLOTS)]
        h3hi = [sb(f"h3hi_{q}", [P, P], F32R) for q in range(2)]
        h3lo = [sb(f"h3lo_{q}", [P, P], F32R) for q in range(2)]
        r = h1T
        rT = h2T
        stf = [sb(f"stf_{q}", [P, 6]) for q in range(2)]
        mve = [sb(f"mve_{q}", [P, 2, 2]) for q in range(2)]
        sde = [sb(f"sde_{q}", [P, 2]) for q in range(2)]
        rse = [sb(f"rse_{q}", [P, 2]) for q in range(2)]
        v0 = [wmod[:, n * D:(n + 1) * D] for n in range(2)]
        v = [sb(f"v_{q}", [P, D]) for q in range(2)]
        sty = [sb(f"sty_{q}", [P, 6]) for q in range(2)]
        vg = [sb(f"vg_{q}", [P, D]) for q in range(2)]
        vs = [wmod[:, (2 + n) * D:(3 + n) * D] for n in range(2)]
        y = [sb(f"y_{q}", [P, D]) for q in range(2)]
        targets = sb("targets", [P, EXPERT_TILES], I32)
        target = [sb(f"target_{q}", [P, 1], I32) for q in range(2)]
        gate = sb("gate", [P, TOPK, NT])
        Y_SLOTS = 8
        y01 = [t[:, 0:J * TOPK * D].rearrange("p (j k) -> p j k", j=J) for t in (
            [W2[:].rearrange("p e d -> p (e d)")[:, n * J * TOPK * D:(n + 1) * J * TOPK * D] for n in range(4)] +
            [t[:].rearrange("p c l -> p (c l)") for t in xi] + [t[:].rearrange("p e i -> p (e i)") for t in (past, hop)])]
        y0g = n1
        ysum = n2
        ygb = [t[:, :].rearrange("p (j d) -> p j d", j=J) for t in scan]

        XL = B // 2
        x_loaded = [sem(f"x_loaded{n}") for n in range(XL)]
        small_loaded = sem("small_loaded")
        mod_loaded = sem("mod_loaded")
        w1_loaded = [sem(f"w1_loaded{q}") for q in range(2)]
        w2_loaded, gains_loaded, rows_loaded = (
            sem("w2_loaded"), sem("gains_loaded"), sem("rows_loaded"))
        b2_loaded = sem("b2_loaded")
        w1hi_ready, w1lo_ready = sem("w1hi_ready"), sem("w1lo_ready")
        spare_stored = sem("spare_stored")
        pool_consts = sem("pool_consts")
        dve_setup, act_setup, pe_setup = sem("dve_setup"), sem("act_setup"), sem("pe_setup")
        gb_stored, gb_loaded, b1_stored = sem("gb_stored"), sem("gb_loaded"), sem("b1_stored")
        (n1_ready, t1_done, h1T_ready, xi0_done, xi1_done, xi0_ready, xi1_ready, z_done, u_done, skip_ready,
         scan_ready, mix_ready, mix_done) = [sem(n) for n in (
             "n1_ready", "t1_done", "h1T_ready", "xi0_done", "xi1_done", "xi0_ready", "xi1_ready", "z_done",
             "u_done", "skip_ready", "scan_ready", "mix_ready", "mix_done")]
        (x1_ready, n2_ready, t2_done, h2T_ready, back_done, logit_done, rows_ready, logit_ready, best_ready,
         besti_ready, hot_ready, hots_ready, carry_ready, rank_done, place_ready, placed_ready, slot_ready,
         hotsum_ready, ids_ready) = [sem(n) for n in (
             "x1_ready", "n2_ready", "t2_done", "h2T_ready", "back_done", "logit_done", "rows_ready", "logit_ready",
             "best_ready", "besti_ready", "hot_ready", "hots_ready", "carry_ready", "rank_done", "place_ready",
             "placed_ready", "slot_ready", "hotsum_ready", "ids_ready")]
        mv_ready, ve_ready, guess_ready, nm_ready = [sem(n) for n in ("mv_ready", "ve_ready", "guess_ready", "nm_ready")]
        newton = [[sem(f"{what}{n}_ready") for what in ("sq", "hv", "rs")] for n in range(3)]
        stats_ready, first_stats_ready = sem("stats_ready"), sem("first_stats_ready")
        rows_stored = [sem(f"rows_stored{q}") for q in range(2)]
        sums_done, sums_copied, sums_stored, sums_loaded, w2_ready = (
            sem("sums_done"), sem("sums_copied"), sem("sums_stored"), sem("sums_loaded"), sem("w2_ready"))
        count_done, table_step, table_ready, padding_stored = (
            sem("count_done"), sem("table_step"), sem("table_ready"), sem("padding_stored"))
        hrow_loaded = [sem(f"hrow_loaded{n}") for n in range(SLOTS)]
        (t3_done, h3hi_ready, h3lo_ready, h_done, r_ready, tr_done, rT_ready, y_done, stf_ready, v0_ready, v_ready, sty_ready,
         vg_ready, vs_ready, y_ready, targets_ready, target_ready) = [sem(n) for n in (
             "t3_done", "h3hi_ready", "h3lo_ready", "h_done", "r_ready", "tr_done", "rT_ready", "y_done", "stf_ready", "v0_ready",
             "v_ready", "sty_ready", "vg_ready", "vs_ready", "y_ready", "targets_ready", "target_ready")]
        mve_ready, sde_ready, rse_ready = sem("mve_ready"), sem("sde_ready"), sem("rse_ready")
        results_stored = [sem(f"results_stored{q}") for q in range(2)]
        gate_ready = sem("gate_ready")
        y01_loaded = [sem(f"y01_loaded{n}") for n in range(Y_SLOTS)]
        y0g_ready, ysum_ready, ygb_ready, o_ready = (
            sem("y0g_ready"), sem("ysum_ready"), sem("ygb_ready"), sem("o_ready"))
        out_stored = sem("out_stored")

        block = ctx.enter_context(nc.Block())

        PER = 16 * J * TOPK

        def on(i, n):
            return not isinstance(i, int) or 0 <= i < n

        FIRST1, LOOP1, LAST1 = -2, (6, B - 2), B + 2
        TURN = 8
        FIRST2, LOOP2, LAST2 = -1, (8, (EXPERT_TILES - 2) // TURN * TURN), EXPERT_TILES + 5
        assert B % 2 == 0 and E == B // 2

        def norms(s):
            return slice(0 if on(s - 1, EXPERT_TILES) else 1, 2 if on(s - 4, EXPERT_TILES) else 1)

        def run(engine, step, first, loop, last):
            for s in range(first, loop[0]):
                step(s, s % 2, s // 2)
            with engine.Fori(loop[0] // 2, loop[1] // 2) as pair:
                step(pair * 2, 0, pair)
                step(pair * 2 + 1, 1, pair)
            for s in range(loop[1], last + 1):
                step(s, s % 2, s // 2)

        def run_tiles(engine, step, name=None, experts=None, oldest=0):
            def load(start, count):
                if experts is None:
                    return None
                _, values = nc.values_load_multi_w_load_instructions(
                    experts[0:1, bass.ds(start + -oldest % 4, count)], engines=(name,), min_val=0, max_val=E - 1,
                    skip_runtime_bounds_check_because="a count of experts, cut off at E - 1")
                return values

            def peeled(begin, end):
                start = max(begin + oldest, 0)
                loaded = load(start, min(end + oldest + 2, EXPERT_TILES) - start)
                for s in range(begin, end):
                    step(s, s % TURN, lambda k: loaded[s + k - start])

            peeled(FIRST2, LOOP2[0])
            with engine.Fori(LOOP2[0] // TURN, LOOP2[1] // TURN) as turn:
                loaded = load(turn * TURN + oldest, TURN + 2)
                for n in range(TURN):
                    step(turn * TURN + n, n, lambda k: loaded[k - oldest + n])
            peeled(LOOP2[1], LAST2 + 1)

        def wide(ap):
            return ap.rearrange("p (o d) -> p o d", o=1)

        def tiles(b):
            return bass.ds(b * J, J)

        @block.sync
        def _(sp):
            sp.dma_start(c_sb[:], c_in).then_inc(mod_loaded, 16)
            sp.dma_start(wmod[:], wmod_in).then_inc(mod_loaded, 16)
            NX = NT // XL
            sp.dma_start(X[:, 0:NX, :], x_v[:, 0:NX, :]).then_inc(x_loaded[0], 16)
            sp.dma_start(g1r[:], g1_in.rearrange("e (c p) -> (e c) p", p=P)).then_inc(gains_loaded, 16)
            sp.dma_start(be1r[:], be1_in.rearrange("e (c p) -> (e c) p", p=P)).then_inc(gains_loaded, 16)
            sp.dma_start(b1f[:], b1_in).then_inc(gains_loaded, 16)
            sp.dma_start(W2[:], w2_in.rearrange("e (c p) d -> p (e c) d", p=P)).then_inc(w2_loaded, 16)
            sp.dma_start(win[:], win_in).then_inc(small_loaded, 16)
            sp.dma_start(wout[:], wout_in.rearrange("(c p) d -> p c d", p=P)).then_inc(small_loaded, 16)
            sp.dma_start(bp[:], bp_in.rearrange("(c p) s -> p c s", p=P)).then_inc(small_loaded, 16)
            sp.dma_start(cp[:], cp_in).then_inc(small_loaded, 16)
            sp.dma_start(bcol[:], bin_in.rearrange("(c p) -> p c", p=P), allow_slow_non_contiguous=True).then_inc(small_loaded, 16)
            sp.dma_start(dcol[:], dp_in.rearrange("(c p) -> p c", p=P), allow_slow_non_contiguous=True).then_inc(small_loaded, 16)
            sp.dma_start(boutc[:], bout_in.rearrange("(p o) -> p o", o=1), allow_slow_non_contiguous=True).then_inc(small_loaded, 16)
            sp.dma_start(wr[:], wr_in).then_inc(small_loaded, 16)
            sp.dma_start(br[:], br_in.rearrange("(o e) -> o e", o=1).broadcast_to([P, E])).then_inc(small_loaded, 16)
            sp.dma_start(X[:, NX:2 * NX, :], x_v[:, NX:2 * NX, :]).then_inc(x_loaded[1], 16)

            def on_every_partition(src):
                return src.rearrange("(o e) d -> o e d", o=1).broadcast_to([P, E, D])

            def load_w1(n):
                if n >= 2:
                    sp.wait_ge(w1lo_ready, n - 1)
                sp.dma_start(w1_raw[n % 2], w1_in[n * W1E:(n + 1) * W1E].rearrange("e p f -> p e f")).then_inc(w1_loaded[n % 2], 16)

            load_w1(0)
            load_w1(1)
            sp.wait_ge(pool_consts, 7)
            sp.dma_start(b2_rows[0:1, :, :], b2_in.rearrange("(o e) d -> o e d", o=1)).then_inc(b2_loaded, 16)
            for n in range(2, XL):
                sp.dma_start(X[:, n * NX:(n + 1) * NX, :], x_v[:, n * NX:(n + 1) * NX, :]).then_inc(x_loaded[n], 16)
            for n in range(2, E // W1E):
                load_w1(n)
            sp.dma_start(g2[:], on_every_partition(g2_in)).then_inc(rows_loaded, 16)
            sp.dma_start(be2[:], on_every_partition(be2_in)).then_inc(rows_loaded, 16)
            sp.wait_ge(dve_setup, SETUP_GB)
            sp.dma_start(gates_d.rearrange("o (b d) -> (o b) d", b=B), gb_raw[:]).then_inc(gb_stored, 16)
            sp.wait_ge(sums_copied, 1)
            sp.dma_start(sums_d, w2_sums).then_inc(sums_stored, 16)
            sp.wait_ge(sums_stored, 16)
            for to, row in ((c2[:], 0), (means[:, 0:E, :], 1)):
                sp.dma_start(to, sums_d[row:row + 1].broadcast_to([P, E, D])).then_inc(sums_loaded, 16)
            sp.wait_ge(dve_setup, SETUP_END)
            sp.wait_ge(act_setup, 2)
            sp.dma_start(b1_parts[0:1, :, :].bitcast(F32), b1hi[:].bitcast(F32)).then_inc(b1_stored, 16)
            sp.dma_start(b1_parts[1:2, :, :].bitcast(F32), b1lo[:].bitcast(F32)).then_inc(b1_stored, 16)
            sp.wait_ge(dve_setup, SETUP_PADDING)
            for n in range(NSPARE):
                sp.dma_start(rows_d[SPARE + n * P:SPARE + (n + 1) * P, :], padding[:]).then_inc(spare_stored, 16)
            sp.wait_ge(table_step, 1)
            for e in range(E):
                n = sp.value_load(cnt_i[0:1, e:e + 1], min_val=0, max_val=T)
                sp.dma_start(rows_d[bass.ds(n + e * REGION, P), :], padding[:]).then_inc(padding_stored, 16)
            sp.wait_ge(table_ready, 1)
            starts = [sp.value_load(tile_row[0:1, n:n + 1], min_val=0, max_val=SPARE + (NSPARE - 1) * P) for n in range(SLOTS)]
            sp.wait_ge(spare_stored, 16 * NSPARE)
            sp.wait_ge(padding_stored, 16 * E)
            for q in range(2):
                sp.wait_ge(rows_stored[q], 16 * J * TOPK * (B // 2))

            def load_rows(i, n, start):
                sp.dma_start(hrow[n], rows_d[bass.ds(start, P), :]).then_inc(hrow_loaded[n], 16)

            def first_row(i):
                return sp.value_load(tile_row[0:1, bass.ds(i, 1)], min_val=0, max_val=SPARE + (NSPARE - 1) * P)

            def load_next(i, n):
                start = first_row(i)
                sp.wait_ge(t3_done, i - 3)
                sp.wait_ge(targets_ready, i - 3)
                load_rows(i, n, start)

            for n in range(SLOTS):
                load_rows(n, n, starts[n])
            sp.wait_ge(gb_stored, 16)
            sp.wait_ge(w2_ready, 1)
            sp.dma_start(gb_rows[:], gates_d.rearrange("o (b d) -> o b d", b=B).broadcast_to([P, B, D])).then_inc(gb_loaded, 16)
            with sp.Fori(1, EXPERT_TILES // SLOTS) as turn:
                for n in range(SLOTS):
                    load_next(turn * SLOTS + n, n)
            for i in range(EXPERT_TILES // SLOTS * SLOTS, EXPERT_TILES):
                load_next(i, i % SLOTS)
            for q in range(2):
                sp.wait_ge(results_stored[q], 16 * ((EXPERT_TILES + 1 - q) // 2))

            def load_results(b, n):
                sp.dma_start(y01[n], results_v[:, tiles(b), :]).then_inc(y01_loaded[n], 16)

            def store_out(b):
                sp.wait_ge(o_ready, b + 1)
                sp.dma_start(out_v[:, tiles(b), :], X[:, tiles(b), :]).then_inc(out_stored, 16)

            for n in range(Y_SLOTS):
                load_results(n, n)
            with sp.Fori(1, B // Y_SLOTS) as turn:
                for n in range(Y_SLOTS):
                    b = turn * Y_SLOTS + n
                    sp.wait_ge(ysum_ready, b - Y_SLOTS + 1)
                    load_results(b, n)
                    store_out(b - Y_SLOTS)
            for n in range(Y_SLOTS):
                store_out(B - Y_SLOTS + n)
            sp.wait_ge(out_stored, 16 * B)

        @block.gpsimd
        def _(pool):
            nc.gpsimd.iota(offs[:], pattern=[[1, P]], base=0, channel_multiplier=-1).then_inc(pool_consts, 1)
            nc.gpsimd.iota(iota_ei[:], pattern=[[1, E]], base=0, channel_multiplier=0).then_inc(pool_consts, 1)
            nc.gpsimd.iota(token_i[:], pattern=[[TOPK * P, NT]], base=0, channel_multiplier=TOPK).then_inc(pool_consts, 1)
            nc.gpsimd.iota(it_i[:], pattern=[[1, EXPERT_TILES]], base=0, channel_multiplier=0).then_inc(pool_consts, 1)
            nc.gpsimd.memset(decay[:], DECAY).then_inc(pool_consts, 1)
            nc.gpsimd.memset(ones[:], 1.0).then_inc(pool_consts, 1)
            nc.gpsimd.memset(b2_rows, 0.0).then_inc(pool_consts, 1)
            pool.wait_ge(pool_consts, 7)
            for n in range(E // W1E):
                part = slice(n * W1E, (n + 1) * W1E)
                pool.wait_ge(w1_loaded[n % 2], n // 2 * 16 + 16)
                nc.gpsimd.tensor_copy(W1hi[:, part, :], w1_raw[n % 2]).then_inc(w1hi_ready, 1)
                pool.wait_ge(w1hi_ready, n + 1)
                nc.gpsimd.tensor_tensor(W1lo[:, part, :], w1_raw[n % 2], W1hi[:, part, :], ALU.subtract).then_inc(w1lo_ready, 1)

            def store_rows(b, q):
                pool.wait_ge(rows_ready, b + 1)
                pool.wait_ge(ids_ready, b + 1)
                pool.wait_ge(slot_ready, b + 1)
                pool.nop(nofuse=True)
                for j in range(J):
                    for k in range(TOPK):
                        nc.gpsimd.indirect_dma_start(
                            out=rows_d, out_offset=bass.IndirectOffsetOnAxis(ap=slot[q][:, j, k:k + 1], axis=0),
                            in_=rows[q][:, j, :], in_offset=None).then_inc(rows_stored[q], 16)

            with pool.Fori(0, B - 1, 2) as b:
                for q in range(2):
                    store_rows(b + q, q)

            def store_results(i, n, first, expert):
                q = n % 2
                pool.wait_ge(targets_ready, i + 1)
                if not first:
                    pool.wait_ge(results_stored[q], (i - q) * 8)
                nc.gpsimd.tensor_copy(target[q][:], targets[:, bass.ds(i, 1)]).then_inc(target_ready, 1)
                pool.wait_ge(vs_ready, i + 1)
                nc.gpsimd.tensor_tensor(wide(y[q][:]), wide(vs[q]), be2[:, bass.ds(expert, 1), :], ALU.add).then_inc(y_ready, 1)
                pool.wait_ge(target_ready, i + 1)
                pool.wait_ge(y_ready, i + 1)
                pool.nop(nofuse=True)
                nc.gpsimd.indirect_dma_start(
                    out=results_d, out_offset=bass.IndirectOffsetOnAxis(ap=target[q][:], axis=0),
                    in_=y[q][:], in_offset=None, bounds_check=TOPK * T - 1, oob_is_err=False,
                ).then_inc(results_stored[q], 16)

            pool.wait_ge(rows_loaded, 32)
            pool.wait_ge(table_ready, 1)

            def turn_of_results(turn, count, first):
                _, expert = nc.values_load_multi_w_load_instructions(
                    pool_experts[0:1, bass.ds(turn * TURN, count)], engines=(mybir.EngineType.Pool,), min_val=0,
                    max_val=E - 1, skip_runtime_bounds_check_because="a count of experts, cut off at E - 1")
                for n in range(count):
                    store_results(turn * TURN + n, n, first and n < 2, expert[n])

            turn_of_results(0, TURN, True)
            with pool.Fori(1, EXPERT_TILES // TURN) as turn:
                turn_of_results(turn, TURN, False)
            turn_of_results(EXPERT_TILES // TURN, EXPERT_TILES % TURN, False)

            with pool.Fori(0, B // 2) as pair:
                for q in range(2):
                    b = pair * 2 + q
                    pool.wait_ge(ygb_ready, b + 1)
                    nc.gpsimd.tensor_tensor(X[:, tiles(b), :], ygb[q][:], X[:, tiles(b), :], ALU.add).then_inc(o_ready, 1)

        @block.scalar
        def _(act):
            act.wait_ge(mod_loaded, 32)
            nc.scalar.activation(c_act[:], c_sb[:], ACT.Silu).then_inc(act_setup, 1)
            act.wait_ge(gains_loaded, 48)
            act.wait_ge(dve_setup, SETUP_PADDING)
            nc.scalar.activation(b1hi[:], b1f[:], ACT.Copy).then_inc(act_setup, 1)
            nc.scalar.activation(onesr[:], onesf[:], ACT.Copy).then_inc(act_setup, 1)

            def normalise(b, dst, x_tiles, rs_, nm_, ready):
                for j in range(J):
                    ins = nc.scalar.activation(dst[:, j:j + 1, :], X[:, bass.ds(b * J + j, 1), :], ACT.Identity,
                                               bias=nm_[:, x_tiles + j:x_tiles + j + 1],
                                               scale=rs_[:, x_tiles + j:x_tiles + j + 1])
                ins.then_inc(ready, 1)

            def mixer_step(s, q, e):
                if on(s - 2, B):
                    act.wait_ge(nm_ready, s + 2)
                    normalise(s - 2, n2[q], 0, rs[1 - q], nm[1 - q], n2_ready)
                if on(s, B):
                    act.wait_ge(xi0_done, s + 1)
                    nc.scalar.activation(xi[q][:, 0, :], bank[1][:], ACT.Silu, bias=bcol[:, 0:1]).then_inc(xi0_ready, 1)
                    act.wait_ge(xi1_done, s + 1)
                    nc.scalar.activation(xi[q][:, 1, :], bank[2][:], ACT.Silu, bias=bcol[:, 1:2]).then_inc(xi1_ready, 1)
                if on(s - 2, B):
                    act.wait_ge(t2_done, s - 1)
                    nc.scalar.activation(h2T[q][:], bank[6][:], ACT.Identity, bias=mod[:, 3, bass.ds(s - 2, 1)],
                                         scale=mod[:, 4, bass.ds(s - 2, 1)]).then_inc(h2T_ready, 1)
                if on(s + 1, B):
                    act.wait_ge(nm_ready, s + 2)
                    normalise(s + 1, n1[1 - q], J, rs[1 - q], nm[1 - q], n1_ready)
                if on(s, B):
                    act.wait_ge(u_done, s + 1)
                    nc.scalar.activation(skip[q][:], bank[4][:], ACT.Identity, bias=ga_bout[:, bass.ds(s, 1)],
                                         scale=mod[:, 2, bass.ds(s, 1)]).then_inc(skip_ready, 1)
                if isinstance(s, int) and s == -1:
                    act.wait_ge(dve_setup, SETUP_END)
                if on(s + 1, B):
                    act.wait_ge(t1_done, s + 2)
                    nc.scalar.activation(h1T[1 - q][:], bank[0][:], ACT.Identity, bias=mod[:, 0, bass.ds(s + 1, 1)],
                                         scale=mod[:, 1, bass.ds(s + 1, 1)]).then_inc(h1T_ready, 1)
                if on(s - 2, B):
                    act.wait_ge(back_done, s - 1)
                    if on(s - 4, B):
                        act.wait_ge(rows_stored[q], (s - 2 - q) * (PER // 2))
                    nc.scalar.activation(rows[q][:, :, 0:D], bank[6][:].rearrange("p (j d) -> p j d", j=J),
                                         ACT.Copy).then_inc(rows_ready, 1)

            run(act, mixer_step, FIRST1, LOOP1, LAST1)

            act.wait_ge(ids_ready, B)
            nc.scalar.activation(gate[:, 0, :], lead[:], ACT.Sigmoid)
            nc.scalar.activation(gate[:, 1, :], lead[:], ACT.Sigmoid, scale=-1.0).then_inc(gate_ready, 1)

            nc.scalar.activation(root_of_eps[:], eps[:], ACT.Sqrt)

            def expert_step(s, n, _):
                q = n % 2
                if on(s + 1, EXPERT_TILES):
                    act.wait_ge(t3_done, s + 2)
                    nc.scalar.activation(h3hi[1 - q][:], bank[7 - q][:, 0:P], ACT.Copy).then_inc(h3hi_ready, 1)
                if on(s, EXPERT_TILES):
                    act.wait_ge(h_done, s + 1)
                    nc.scalar.activation(r[q][:], bank[1 + q][:], ACT.Relu).then_inc(r_ready, 1)
                if on(s - 3, EXPERT_TILES):
                    act.wait_ge(v0_ready, s - 2)
                    if on(s - 5, EXPERT_TILES):
                        act.wait_ge(vg_ready, s - 4)
                    nc.scalar.activation(v[1 - q][:], v0[1 - q], ACT.Relu).then_inc(v_ready, 1)
                if on(s - 1, EXPERT_TILES):
                    act.wait_ge(tr_done, s)
                    nc.scalar.activation(rT[1 - q][:], bank[3 * q][:], ACT.Copy).then_inc(rT_ready, 1)
                if on(s - 6, EXPERT_TILES):
                    act.wait_ge(vg_ready, s - 5)
                    act.wait_ge(rse_ready, s - 2)
                    if on(s - 8, EXPERT_TILES):
                        act.wait_ge(y_ready, s - 7)
                    nc.scalar.activation(vs[q], vg[q][:], ACT.Copy, scale=rse[q][:, 1:2]).then_inc(vs_ready, 1)
                if on(s - 1, EXPERT_TILES) or on(s - 4, EXPERT_TILES):
                    both = norms(s)
                    act.wait_ge(mve_ready, s)
                    nc.scalar.activation(sde[q][:, both], mve[q][:, both, 1], ACT.Sqrt, bias=eps[:]).then_inc(sde_ready, 1)

            run_tiles(act, expert_step)

            def gate_first(b, n, loaded, first):
                q = n % 2
                act.wait_ge(y01_loaded[n], loaded)
                if not first:
                    act.wait_ge(ysum_ready, b - 1)
                for j in range(J):
                    ins = nc.scalar.activation(y0g[q][:, j, :], y01[n][:, j, 0:D], ACT.Copy,
                                               scale=gate[:, 0, bass.ds(b * J + j, 1)])
                ins.then_inc(y0g_ready, 1)

            for n in range(Y_SLOTS):
                gate_first(n, n, 16, n < 2)
            with act.Fori(1, B // Y_SLOTS) as turn:
                for n in range(Y_SLOTS):
                    gate_first(turn * Y_SLOTS + n, n, turn * 16 + 16, False)

        @block.vector
        def _(dve):
            vec = nc.vector
            done = [0]

            def mark(ins):
                ins.then_inc(dve_setup, 1)
                done[0] += 1

            dve.wait_ge(pool_consts, 6)
            vec.tensor_scalar(ident[:], offs[:], 0.0, None, ALU.is_equal)
            vec.tensor_scalar(before[:], offs[:], 0.0, None, ALU.is_gt)
            vec.tensor_copy(iota_e[:], iota_ei[:])
            vec.tensor_scalar(base_e[:], iota_ei[:], float(REGION), None, ALU.mult)
            vec.tensor_copy(token[:], token_i[:])
            vec.tensor_copy(it_f[:], it_i[:])
            vec.memset(carry[:], 0.0)
            vec.memset(onesf[:], 1.0)
            vec.memset(ones_e[:], 1.0)
            vec.memset(eps[:], EPS)
            mark(vec.memset(padding[:], 0.0))
            dve.wait_ge(dve_setup, 1)
            mark(vec.memset(padding[:, D:D + 1], NOWHERE))
            assert done[0] == SETUP_PADDING
            dve.wait_ge(pe_setup, 1)
            mark(vec.tensor_copy(cT[:], bank[0][:, 0:B]))
            assert done[0] == SETUP_CT
            dve.wait_ge(pe_setup, 2)
            m = bank[1][:, 0:5 * B].rearrange("p (m b) -> p m b", m=5)
            vec.tensor_copy(mod[:, 0, :], m[:, 0, :])
            vec.tensor_scalar(mod[:, 1, :], m[:, 1, :], 1.0, None, ALU.add)
            vec.tensor_copy(mod[:, 3, :], m[:, 3, :])
            vec.tensor_scalar(mod[:, 4, :], m[:, 4, :], 1.0, None, ALU.add)
            vec.tensor_scalar(mod_sign[:], m[:, 2, :], 0.0, 2.0, ALU.is_ge, ALU.mult)
            mark(vec.tensor_scalar(gb_sign[:], bank[2][0:B, 0:D], 0.0, 2.0, ALU.is_ge, ALU.mult))
            dve.wait_ge(dve_setup, 4)
            vec.tensor_scalar(mod_sign[:], mod_sign[:], -1.0, None, ALU.add)
            mark(vec.tensor_scalar(gb_sign[:], gb_sign[:], -1.0, None, ALU.add))
            dve.wait_ge(dve_setup, 5)
            vec.tensor_tensor(mod_abs[:], mod_sign[:], m[:, 2, :], ALU.mult)
            mark(vec.tensor_tensor(gb_abs[:], gb_sign[:], bank[2][0:B, 0:D], ALU.mult))
            dve.wait_ge(dve_setup, 6)
            vec.scalar_tensor_tensor(mod[:, 2, :], mod_abs[:], 0.25, mod_sign[:], ALU.max, ALU.mult)
            mark(vec.scalar_tensor_tensor(gb_raw[:], gb_abs[:], 0.25, gb_sign[:], ALU.max, ALU.mult))
            assert done[0] == SETUP_GB
            dve.wait_ge(pe_setup, 3)
            vec.tensor_copy(g1T[:], bank[4][:, 0:E * CF])
            vec.tensor_scalar(be1_g1m[:, :, 1], bank[4][:, 0:E * CF], 1.0 / F, None, ALU.mult)
            mark(vec.tensor_copy(be1_g1m[:, :, 0], bank[4][:, E * CF:2 * E * CF]))
            assert done[0] == SETUP_SUMS
            dve.wait_ge(act_setup, 2)
            mark(vec.tensor_tensor(b1lo[:], b1f[:], b1hi[:], ALU.subtract))

            def mixer_step(s, q, e):
                p = 1 - q
                both = slice(0 if on(s - 1, B) else J, 2 * J if on(s + 2, B) else J)
                a, b, c = s - 1, s + 2, s - 3
                any_norm = on(a, B) or on(b, B)
                if on(a, B):
                    dve.wait_ge(z_done, s)
                    vec.tensor_tensor_scan(scan[p][:], decay[:], bank[3][:], 0.0, ALU.mult, ALU.add).then_inc(scan_ready, 1)
                if on(b, B):
                    if isinstance(b, int):
                        for n in range(XL):
                            if b * J * XL // NT == n or (b == LOOP1[0] + 1 and n > 0):
                                dve.wait_ge(x_loaded[n], 16)
                    for j in range(J):
                        ins = vec.bn_stats(st[q][:, J + j, :], X[:, bass.ds(b * J + j, 1), :])
                    ins.then_inc(first_stats_ready, 1)
                if on(c, B):
                    dve.wait_ge(logit_done, c + 1)
                    vec.tensor_tensor(logit[p][:], bank[7][:, 0:J * E].rearrange("p (j e) -> p j e", j=J),
                                      br[:].rearrange("p (o e) -> p o e", o=1).broadcast_to([P, J, E]),
                                      ALU.add).then_inc(logit_ready, 1)
                if on(a, B):
                    dve.wait_ge(skip_ready, s)
                    dve.wait_ge(scan_ready, s)
                    vec.scalar_tensor_tensor(mixT[p][:], scan[p][:], mod[:, 2, bass.ds(a, 1)], skip[p][:],
                                             ALU.mult, ALU.add).then_inc(mix_ready, 1)
                if on(c, B):
                    dve.wait_ge(logit_ready, c + 1)
                    dve.nop(nofuse=True)
                    for j in range(J):
                        ins = vec.max(best[p][:, j, :], logit[p][:, j, :])
                    ins.then_inc(best_ready, 1)
                if on(b, B):
                    dve.wait_ge(first_stats_ready, b + 1)
                    dve.nop(nofuse=True)
                    for j in range(J, 2 * J):
                        ins = vec.bn_aggr(mv[q][:, j, :], st[q][:, j, :])
                    if not on(a, B):
                        ins.then_inc(mv_ready, 1)
                if on(c, B):
                    dve.wait_ge(best_ready, c + 1)
                    dve.nop(nofuse=True)
                    for j in range(J):
                        ins = vec.max_index(besti[p][:, j, :], best[p][:, j, :], logit[p][:, j, :])
                    ins.then_inc(besti_ready, 1)
                if on(c, B):
                    dve.wait_ge(besti_ready, c + 1)
                    vec.tensor_tensor(
                        hot[p][:], iota_e[:].rearrange("p (a b e) -> p a b e", a=1, b=1).broadcast_to([P, J, TOPK, E]),
                        besti[p][:, :, 0:TOPK].rearrange("p j (k o) -> p j k o", o=1).broadcast_to([P, J, TOPK, E]),
                        ALU.is_equal).then_inc(hot_ready, 1)
                    vec.tensor_tensor(lead[:, tiles(c)], best[p][:, :, 0], best[p][:, :, 1], ALU.subtract)
                    if on(c - 2, B):
                        dve.wait_ge(rows_stored[p], (c - p) * (PER // 2))
                    vec.tensor_copy(rows[p][:, :, D], token[:, tiles(c)])
                    dve.wait_ge(hot_ready, c + 1)
                    vec.tensor_tensor(hots[p][:], hot[p][:, :, 0, :], hot[p][:, :, 1, :], ALU.add).then_inc(hots_ready, 1)
                    vec.tensor_copy(rows[p][:, :, D + 1], besti[p][:, :, 0]).then_inc(ids_ready, 1)
                if on(a, B):
                    xa = X[:, tiles(a), :]
                    dve.wait_ge(mix_done, s)
                    vec.tensor_tensor(xa, xa, bank[5][:].rearrange("p (j d) -> p j d", j=J), ALU.add).then_inc(x1_ready, 1)
                if on(a, B):
                    dve.wait_ge(x1_ready, s)
                    dve.nop(nofuse=True)
                    for j in range(J):
                        ins = vec.bn_stats(st[q][:, j, :], X[:, bass.ds(a * J + j, 1), :])
                    ins.then_inc(stats_ready, 1)
                def square(n):
                    if any_norm:
                        dve.wait_ge(newton[n - 1][2] if n else guess_ready, s + 3)
                        vec.tensor_tensor(sq[q][:, both], rs[q][:, both], rs[q][:, both], ALU.mult).then_inc(newton[n][0], 1)

                def times_v(n):
                    if any_norm:
                        dve.wait_ge(newton[n][0], s + 3)
                        vec.scalar_tensor_tensor(hv[q][:, both], sq[q][:, both], -0.5, ve[q][:, both], ALU.mult,
                                                 ALU.mult).then_inc(newton[n][1], 1)

                def refine(n):
                    if any_norm:
                        dve.wait_ge(newton[n][1], s + 3)
                        vec.scalar_tensor_tensor(rs[q][:, both], hv[q][:, both], 1.5, rs[q][:, both], ALU.add,
                                                 ALU.mult).then_inc(newton[n][2], 1)

                if on(a, B):
                    dve.wait_ge(stats_ready, s)
                    dve.nop(nofuse=True)
                    for j in range(J):
                        ins = vec.bn_aggr(mv[q][:, j, :], st[q][:, j, :])
                    ins.then_inc(mv_ready, 1)
                if on(c, B):
                    dve.wait_ge(hots_ready, c + 1)
                    vec.tensor_reduce(hotsum[p][:], hots[p][:].rearrange("p j e -> p e j"), axis=AX,
                                      op=ALU.add).then_inc(hotsum_ready, 1)
                if any_norm:
                    dve.wait_ge(mv_ready, s + 3)
                    vec.tensor_scalar(ve[q][:, both], mv[q][:, both, 1], EPS, None, ALU.add).then_inc(ve_ready, 1)
                if any_norm:
                    dve.wait_ge(ve_ready, s + 3)
                    if on(s, B):
                        dve.wait_ge(n1_ready, s + 1)
                    if on(s - 3, B):
                        dve.wait_ge(n2_ready, s - 2)
                    vec.tensor_scalar(rs[q][:, both].bitcast(I32), ve[q][:, both].bitcast(I32), -0.5, float(0x5F3759DF),
                                      ALU.mult, ALU.add).then_inc(guess_ready, 1)
                square(0)
                times_v(0)
                refine(0)
                if on(c, B):
                    dve.wait_ge(rank_done, c + 1)
                    vec.tensor_tensor(place[p][:], bank[7][:, J * E:2 * J * E].rearrange("p (j e) -> p j e", j=J),
                                      base_e[:].rearrange("p (o e) -> p o e", o=1).broadcast_to([P, J, E]),
                                      ALU.add).then_inc(place_ready, 1)
                square(1)
                if on(c, B):
                    dve.wait_ge(hotsum_ready, c + 1)
                    vec.tensor_tensor(carry[:], carry[:], hotsum[p][:], ALU.add).then_inc(carry_ready, 1)
                times_v(1)
                if on(c, B):
                    dve.wait_ge(place_ready, c + 1)
                    vec.tensor_tensor(placed[p][:], hot[p][:],
                                      place[p][:].rearrange("p j (o e) -> p j o e", o=1).broadcast_to([P, J, TOPK, E]),
                                      ALU.mult).then_inc(placed_ready, 1)
                refine(1)
                square(2)
                if on(c, B):
                    dve.wait_ge(placed_ready, c + 1)
                    with nc.allow_low_precision(reason="one whole number below 2**24 and zeros"):
                        vec.tensor_reduce(slot[p][:], placed[p][:], axis=AX, op=ALU.add).then_inc(slot_ready, 1)
                times_v(2)
                refine(2)
                if any_norm:
                    dve.wait_ge(newton[2][2], s + 3)
                    vec.scalar_tensor_tensor(nm[q][:, both], mv[q][:, both, 0], -1.0, rs[q][:, both], ALU.mult,
                                             ALU.mult).then_inc(nm_ready, 1)
                if isinstance(s, int) and s == 0:
                    dve.wait_ge(sums_done, 1)
                    dve.wait_ge(b2_loaded, 16)
                    for half in range(2):
                        part = slice(half * E // 2, (half + 1) * E // 2)
                        ins = vec.tensor_tensor(w2_sums[:, part, :], bank[6 + half][0:2, :].rearrange("k (e d) -> k e d", d=D),
                                                b2_rows[:, part, :], ALU.add)
                    ins.then_inc(sums_copied, 1)

            mixer_step(FIRST1, 0, FIRST1 // 2)
            dve.wait_ge(dve_setup, 7)
            dve.wait_ge(small_loaded, 16 * 9)
            vec.tensor_scalar(ga_bout[:], mod[:, 2, :], boutc[:], None, ALU.mult)
            dve.wait_ge(pe_setup, 4)
            mark(vec.tensor_tensor(cpT[:], bank[3][:, 0:CI * NS].rearrange("p (c s) -> p c s", c=CI), bp[:], ALU.mult))
            dve.wait_ge(dve_setup, 10)
            mark(vec.tensor_reduce(ccol[:], cpT[:], axis=AX, op=ALU.add))
            dve.wait_ge(dve_setup, 11)
            for ch in range(CI):
                vec.tensor_scalar(wz[:, ch, :], wout[:, ch, :], ccol[:, ch:ch + 1], None, ALU.mult)
                ins = vec.tensor_scalar(wu[:, ch, :], wout[:, ch, :], dcol[:, ch:ch + 1], None, ALU.mult)
            mark(ins)
            assert done[0] == SETUP_END
            run(dve, mixer_step, FIRST1 + 1, LOOP1, LAST1)

            ticks = [0]

            def link(ins):
                ins.then_inc(table_step, 1)
                ticks[0] += 1
                dve.wait_ge(table_step, ticks[0])

            dve.wait_ge(count_done, 1)
            vec.tensor_copy(cnt_i[:], bank[7][:, 0:E])
            link(vec.tensor_scalar(cnt[:], bank[7][:, 0:E], float(P - 1), None, ALU.add))
            link(vec.tensor_copy(nt_i[:], cnt[:]))
            link(vec.tensor_scalar(nt_i[:], nt_i[:], P.bit_length() - 1, None, ALU.logical_shift_right))
            link(vec.tensor_copy(nt_f[:], nt_i[:]))
            vec.tensor_scalar(jump[:], nt_f[:], -float(P), float(REGION), ALU.mult, ALU.add)
            link(vec.tensor_tensor_scan(ends[:], ones_e[:], nt_f[:], 0.0, ALU.mult, ALU.add))
            dve.wait_ge(w1lo_ready, E // W1E)
            for e in range(E):
                vec.tensor_scalar(past[:, e, :], it_f[:], ends[:, e:e + 1], None, ALU.is_ge)
                ins = vec.tensor_scalar(hop[:, e, :], it_f[:], ends[:, e:e + 1], jump[:, e:e + 1], ALU.is_ge, ALU.mult)
            link(ins)
            vec.tensor_reduce(tile_e[:], past[:].rearrange("p e i -> p i e"), axis=AX, op=ALU.add)
            link(vec.tensor_reduce(tile_hop[:], hop[:].rearrange("p e i -> p i e"), axis=AX, op=ALU.add))
            vec.tensor_scalar(pe_experts[:, 2:2 + EXPERT_TILES], tile_e[:], float(E - 1), None, ALU.min)
            vec.tensor_scalar(pool_experts[:], tile_e[:], float(E - 1), None, ALU.min)
            vec.tensor_scalar(dve_experts[:, 1:1 + EXPERT_TILES], tile_e[:], float(E - 1), None, ALU.min)
            vec.scalar_tensor_tensor(tile_row[:], it_f[:], float(P), tile_hop[:], ALU.mult, ALU.add).then_inc(table_ready, 1)
            dve.wait_ge(table_ready, 1)

            dve.wait_ge(sums_loaded, 32)
            for n in range(E * CF):
                ins = vec.scalar_tensor_tensor(W2[:, n, :], W2[:, n, :], g1T[:, n:n + 1], means[:, n // CF, :],
                                               ALU.mult, ALU.subtract)
            ins.then_inc(w2_ready, 1)

            dve.wait_ge(rows_loaded, 32)

            def target_of(i, n):
                dve.wait_ge(hrow_loaded[n], (i + SLOTS - n) * 4)
                vec.scalar_tensor_tensor(targets[:, bass.ds(i, 1)], hrow[n][:, D + 1:D + 2], tile_e[:, bass.ds(i, 1)],
                                         hrow[n][:, D:D + 1], ALU.not_equal, ALU.add).then_inc(targets_ready, 1)

            def expert_step(s, n, expert):
                q, p = n % 2, 1 - n % 2
                if on(s - 3, EXPERT_TILES):
                    e3 = expert(-3)
                    dve.wait_ge(y_done, s - 2)
                    dve.wait_ge(rse_ready, s - 2)
                    vec.scalar_tensor_tensor(wide(v0[p]), wide(bank[4 + p][:, 0:D]), rse[q][:, 0:1],
                                             c2[:, bass.ds(e3, 1), :], ALU.mult, ALU.add).then_inc(v0_ready, 1)
                if on(s - 2, EXPERT_TILES) or on(s - 5, EXPERT_TILES):
                    both = norms(s - 1)
                    dve.wait_ge(sde_ready, s - 1)
                    if on(s - 7, EXPERT_TILES):
                        dve.wait_ge(vs_ready, s - 6)
                    vec.reciprocal(rse[p][:, both], sde[p][:, both]).then_inc(rse_ready, 1)
                if on(s - 5, EXPERT_TILES):
                    e = expert(-5)
                    vec.scalar_tensor_tensor(wide(vg[p][:]), wide(v[p][:]), mve[p][:, 1, 0:1], g2[:, bass.ds(e, 1), :],
                                             ALU.subtract, ALU.mult).then_inc(vg_ready, 1)
                if on(s + 1, EXPERT_TILES):
                    dve.wait_ge(h3hi_ready, s + 2)
                    vec.tensor_tensor(h3lo[p][:], bank[6 + p][:, 0:P], h3hi[p][:], ALU.subtract).then_inc(h3lo_ready, 1)
                if on(s - 4, EXPERT_TILES):
                    dve.wait_ge(v_ready, s - 3)
                    dve.nop(nofuse=True)
                    vec.bn_stats(sty[q][:], v[q][:]).then_inc(sty_ready, 1)
                if on(s - 1, EXPERT_TILES):
                    dve.wait_ge(r_ready, s)
                    dve.nop(nofuse=True)
                    vec.bn_stats(stf[p][:], r[p][:]).then_inc(stf_ready, 1)
                if on(s - 4, EXPERT_TILES):
                    dve.wait_ge(sty_ready, s - 3)
                    dve.nop(nofuse=True)
                    ins = vec.bn_aggr(mve[q][:, 1, :], sty[q][:])
                if on(s + 1, EXPERT_TILES):
                    target_of(s + 1, (n + 1) % SLOTS)
                if on(s - 1, EXPERT_TILES):
                    dve.wait_ge(stf_ready, s)
                    dve.nop(nofuse=True)
                    ins = vec.bn_aggr(mve[q][:, 0, :], stf[p][:])
                if on(s - 1, EXPERT_TILES) or on(s - 4, EXPERT_TILES):
                    ins.then_inc(mve_ready, 1)

            run_tiles(dve, expert_step, mybir.EngineType.DVE, dve_experts, -5)

            dve.wait_ge(gate_ready, 1)
            dve.wait_ge(gb_loaded, 16)

            def sums(b, n, first):
                q = n % 2
                dve.wait_ge(y0g_ready, b + 1)
                for j in range(J):
                    ins = vec.scalar_tensor_tensor(ysum[q][:, j, :], y01[n][:, j, D:2 * D], gate[:, 1, bass.ds(b * J + j, 1)],
                                                   y0g[q][:, j, :], ALU.mult, ALU.add)
                ins.then_inc(ysum_ready, 1)
                dve.wait_ge(ysum_ready, b + 1)
                if not first:
                    dve.wait_ge(o_ready, b - 1)
                vec.tensor_tensor(ygb[q][:], ysum[q][:], gb_rows[:, bass.ds(b, 1), :].broadcast_to([P, J, D]),
                                  ALU.mult).then_inc(ygb_ready, 1)

            for n in range(Y_SLOTS):
                sums(n, n, n < 2)
            with dve.Fori(1, B // Y_SLOTS) as turn:
                for n in range(Y_SLOTS):
                    sums(turn * Y_SLOTS + n, n, False)

        @block.tensor
        def _(pe):
            mm, tr = nc.tensor.matmul, nc.tensor.transpose
            pe.wait_ge(dve_setup, SETUP_PADDING)
            pe.wait_ge(act_setup, 1)
            tr(bank[0][:, 0:B], c_act[:], ident[0:B, 0:B]).then_inc(pe_setup, 1)
            pe.wait_ge(dve_setup, SETUP_CT)
            for n in range(5):
                mm(bank[1][:, n * B:(n + 1) * B], wmod[:, n * D:(n + 1) * D], cT[:], start=True, stop=True)
            mm(bank[2][0:B, 0:D], cT[:], wmod[:, 5 * D:6 * D], start=True, stop=True).then_inc(pe_setup, 1)
            pe.wait_ge(gains_loaded, 48)
            tr(bank[4][:, 0:E * CF], g1r[:], ident[0:E * CF, 0:E * CF])
            tr(bank[4][:, E * CF:2 * E * CF], be1r[:], ident[0:E * CF, 0:E * CF]).then_inc(pe_setup, 1)
            pe.wait_ge(small_loaded, 16 * 9)
            for ch in range(CI):
                ins = tr(bank[3][:, ch * NS:(ch + 1) * NS], cp[:, ch * P:(ch + 1) * P], ident[0:NS, 0:NS])
            ins.then_inc(pe_setup, 1)
            pe.wait_ge(dve_setup, SETUP_SUMS)
            pe.wait_ge(w2_loaded, 16)
            for e in range(E):
                for ch in range(CF):
                    ins = mm(bank[6 + 2 * e // E][0:2, e * D % 512:e * D % 512 + D], be1_g1m[:, e * CF + ch, :],
                             W2[:, e * CF + ch, :], start=(ch == 0), stop=(ch == CF - 1))
            ins.then_inc(sums_done, 1)
            pe.wait_ge(dve_setup, SETUP_END)

            def transpose_batch(to, of):
                for j in range(J):
                    ins = tr(bank[to][:, j * P:(j + 1) * P], of(j), ident[:])
                return ins

            def mixer_step(s, q, e):
                p = 1 - q
                if on(s, B):
                    pe.wait_ge(h1T_ready, s + 1)
                    mm(bank[1][:], win[:, 0:P], h1T[q][:], start=True, stop=True).then_inc(xi0_done, 1)
                    mm(bank[2][:], win[:, P:2 * P], h1T[q][:], start=True, stop=True).then_inc(xi1_done, 1)
                if on(s - 1, B):
                    pe.wait_ge(mix_ready, s)
                    transpose_batch(5, lambda j: mixT[p][:, j * P:(j + 1) * P]).then_inc(mix_done, 1)
                if on(s - 2, B):
                    if isinstance(s, int) and s == 2:
                        pe.wait_ge(sums_copied, 1)
                    pe.wait_ge(n2_ready, s - 1)
                    if on(s - 3, B):
                        pe.wait_ge(rows_ready, s - 2)
                    transpose_batch(6, lambda j: n2[q][:, j, :]).then_inc(t2_done, 1)
                if on(s - 3, B):
                    acc = bank[7][:, J * E:2 * J * E].rearrange("p (j e) -> p j e", j=J)
                    pe.wait_ge(hots_ready, s - 2)
                    mm(acc, before[:], hots[p][:], start=True, stop=False)
                    for j in range(J - 1):
                        mm(acc[:, j + 1:J, :], ones[:], hots[p][:, j:j + 1, :].broadcast_to([P, J - 1 - j, E]),
                           start=False, stop=False)
                    if on(s - 4, B):
                        pe.wait_ge(carry_ready, s - 3)
                    mm(acc, ones[:], carry[:].rearrange("p (o e) -> p o e", o=1).broadcast_to([P, J, E]),
                       start=False, stop=True).then_inc(rank_done, 1)
                if on(s, B):
                    pe.wait_ge(xi0_ready, s + 1)
                    mm(bank[3][:], wz[:, 0, :], xi[q][:, 0, :], start=True, stop=False)
                    pe.wait_ge(xi1_ready, s + 1)
                    mm(bank[3][:], wz[:, 1, :], xi[q][:, 1, :], start=False, stop=True).then_inc(z_done, 1)
                    mm(bank[4][:], wu[:, 0, :], xi[q][:, 0, :], start=True, stop=False)
                    mm(bank[4][:], wu[:, 1, :], xi[q][:, 1, :], start=False, stop=True).then_inc(u_done, 1)
                if on(s + 1, B):
                    pe.wait_ge(n1_ready, s + 2)
                    transpose_batch(0, lambda j: n1[p][:, j, :]).then_inc(t1_done, 1)
                if on(s - 2, B):
                    pe.wait_ge(h2T_ready, s - 1)
                    if on(s - 3, B):
                        pe.wait_ge(place_ready, s - 2)
                    for j in range(J):
                        ins = mm(bank[7][:, j * E:(j + 1) * E], h2T[q][:, j * P:(j + 1) * P], wr[:], start=True, stop=True)
                    ins.then_inc(logit_done, 1)
                    transpose_batch(6, lambda j: h2T[q][:, j * P:(j + 1) * P]).then_inc(back_done, 1)
            run(pe, mixer_step, FIRST1, LOOP1, LAST1)
            pe.wait_ge(carry_ready, B)
            pe.wait_ge(place_ready, B)
            mm(bank[7][:, 0:E], ones[:], carry[:], start=True, stop=True).then_inc(count_done, 1)

            pe.wait_ge(w2_ready, 1)
            pe.wait_ge(w1lo_ready, E // W1E)
            pe.wait_ge(b1_stored, 32)
            pe.wait_ge(table_ready, 1)

            def expert_step(s, n, expert):
                q, p = n % 2, 1 - n % 2
                if on(s + 1, EXPERT_TILES):
                    row_slot = (n + 1) % SLOTS
                    pe.wait_ge(hrow_loaded[row_slot], (s + 1 + SLOTS - row_slot) * 4)
                    tr(bank[6 + p][:, 0:P], hrow[row_slot][:, 0:D], ident[:]).then_inc(t3_done, 1)
                if on(s, EXPERT_TILES):
                    e = expert(0)
                    h = bank[1 + q][:].rearrange("p (o f) -> p o f", o=1)
                    pe.wait_ge(h3lo_ready, s + 1)
                    if on(s - 2, EXPERT_TILES):
                        pe.wait_ge(r_ready, s - 1)
                    mm(h, onesr[:], b1_parts[:, bass.ds(e, 1), :], start=True, stop=False)
                    mm(h, h3hi[q][:], W1hi[:, bass.ds(e, 1), :], start=False, stop=False)
                    mm(h, h3hi[q][:], W1lo[:, bass.ds(e, 1), :], start=False, stop=False)
                    mm(h, h3lo[q][:], W1hi[:, bass.ds(e, 1), :], start=False, stop=True).then_inc(h_done, 1)
                if on(s - 1, EXPERT_TILES):
                    pe.wait_ge(r_ready, s)
                    for ch in range(CF):
                        ins = tr(bank[3 * q][:, ch * P:(ch + 1) * P], r[p][:, ch * P:(ch + 1) * P], ident[:])
                    ins.then_inc(tr_done, 1)
                if on(s - 2, EXPERT_TILES):
                    e2 = expert(-2)
                    acc = bank[4 + q][:, 0:D].rearrange("p (o d) -> p o d", o=1)
                    pe.wait_ge(rT_ready, s - 1)
                    if on(s - 4, EXPERT_TILES):
                        pe.wait_ge(v0_ready, s - 3)
                    for ch in range(CF):
                        ins = mm(acc, rT[q][:, ch * P:(ch + 1) * P], W2[:, bass.ds(e2 * CF + ch, 1), :],
                                 start=(ch == 0), stop=(ch == CF - 1))
                    ins.then_inc(y_done, 1)

            run_tiles(pe, expert_step, mybir.EngineType.PE, pe_experts, -2)


SETUP_PADDING, SETUP_CT, SETUP_GB, SETUP_SUMS, SETUP_END = 2, 3, 7, 8, 12

_INS = ['L0_attn_x', 'L0_attn_Win', 'L0_attn_bin_', 'L0_attn_Bp', 'L0_attn_Cp', 'L0_attn_Dp', 'L0_attn_Wout',
        'L0_attn_bout', 'L0_ffn_Wr', 'L0_ffn_br', 'L0_ffn_W1', 'L0_ffn_b1', 'L0_ffn_g1', 'L0_ffn_be1', 'L0_ffn_W2',
        'L0_ffn_b2', 'L0_ffn_g2', 'L0_ffn_be2', 'L0_c', 'L0_wmod']


def kernel(**inputs):
    import numpy as _np
    import concourse.bacc as _bacc
    from concourse.bass_utils import run_bass_kernel_spmd as _run

    nc = _bacc.Bacc("TRN2", target_bir_lowering=False, num_devices=1)
    arrays, args = {}, []
    for name in _INS:
        a = _np.ascontiguousarray(inputs[name])
        arrays[f"in_{name}"] = a
        args.append(nc.dram_tensor(f"in_{name}", a.shape, mybir.dt.from_np(a.dtype), kind="ExternalInput").ap())
    shape = tuple(inputs['L0_attn_x'].shape)
    args.append(nc.dram_tensor("out_x", shape, mybir.dt.float32, kind="ExternalOutput").ap())
    adaln_ssm_moe_kernel(nc, *args)
    r = _run(nc, [arrays], core_ids=[0])
    return r.results[0]["out_x"]
```
